# Optimizing a Trainium2 kernel written in Bass

```python
import numpy as np
import jax
import jax.numpy as jnp

def _softmax(x, axis=-1):
    return jax.nn.softmax(x, axis=axis)

def _gelu(x):
    return jax.nn.gelu(x, approximate=True)

def _silu(x):
    return jax.nn.silu(x)

def _sigmoid(x):
    return jax.nn.sigmoid(x)

def _layernorm(x, axis=-1, eps=1e-05):
    m = jnp.mean(x, axis=axis, keepdims=True)
    v = jnp.var(x, axis=axis, keepdims=True)
    return (x - m) / jnp.sqrt(v + eps)

def _scatter_add(tgt, idx, src, axis=0):
    return tgt.at[idx].add(src)

def _segment_sum(src, seg, n):
    return jax.ops.segment_sum(src, seg, n)
kernel_name = 'mk_dlrm_tower_d1_rec_r8_0800b3'

def setup_inputs(seed: int=0):
    np.random.seed(seed)
    _w = jnp.asarray

    def _rec_inputs():
        import jax
        import jax.numpy as jnp
        _tk = jax.random.key(seed)
        ids = jnp.stack([jax.random.randint(jax.random.fold_in(_tk, 200 + f), (512,), 0, v, jnp.int32) for f, v in enumerate([1250, 12500, 12500, 1250, 1000, 1000, 12500, 1250, 1250, 1250, 1000, 12500, 1000, 1000, 1000, 125000, 1250, 125000, 1250, 125000, 12500, 12500, 1000, 1000, 12500, 1000])], axis=1)
        tbl_0 = 0.05 * jax.random.normal(jax.random.fold_in(_tk, 500 + 0), (1250, 64), jnp.float32)
        tbl_1 = 0.05 * jax.random.normal(jax.random.fold_in(_tk, 500 + 1), (12500, 64), jnp.float32)
        tbl_2 = 0.05 * jax.random.normal(jax.random.fold_in(_tk, 500 + 2), (12500, 64), jnp.float32)
        tbl_3 = 0.05 * jax.random.normal(jax.random.fold_in(_tk, 500 + 3), (1250, 64), jnp.float32)
        tbl_4 = 0.05 * jax.random.normal(jax.random.fold_in(_tk, 500 + 4), (1000, 64), jnp.float32)
        tbl_5 = 0.05 * jax.random.normal(jax.random.fold_in(_tk, 500 + 5), (1000, 64), jnp.float32)
        tbl_6 = 0.05 * jax.random.normal(jax.random.fold_in(_tk, 500 + 6), (12500, 64), jnp.float32)
        tbl_7 = 0.05 * jax.random.normal(jax.random.fold_in(_tk, 500 + 7), (1250, 64), jnp.float32)
        tbl_8 = 0.05 * jax.random.normal(jax.random.fold_in(_tk, 500 + 8), (1250, 64), jnp.float32)
        tbl_9 = 0.05 * jax.random.normal(jax.random.fold_in(_tk, 500 + 9), (1250, 64), jnp.float32)
        tbl_10 = 0.05 * jax.random.normal(jax.random.fold_in(_tk, 500 + 10), (1000, 64), jnp.float32)
        tbl_11 = 0.05 * jax.random.normal(jax.random.fold_in(_tk, 500 + 11), (12500, 64), jnp.float32)
        tbl_12 = 0.05 * jax.random.normal(jax.random.fold_in(_tk, 500 + 12), (1000, 64), jnp.float32)
        tbl_13 = 0.05 * jax.random.normal(jax.random.fold_in(_tk, 500 + 13), (1000, 64), jnp.float32)
        tbl_14 = 0.05 * jax.random.normal(jax.random.fold_in(_tk, 500 + 14), (1000, 64), jnp.float32)
        tbl_15 = 0.05 * jax.random.normal(jax.random.fold_in(_tk, 500 + 15), (125000, 64), jnp.float32)
        tbl_16 = 0.05 * jax.random.normal(jax.random.fold_in(_tk, 500 + 16), (1250, 64), jnp.float32)
        tbl_17 = 0.05 * jax.random.normal(jax.random.fold_in(_tk, 500 + 17), (125000, 64), jnp.float32)
        tbl_18 = 0.05 * jax.random.normal(jax.random.fold_in(_tk, 500 + 18), (1250, 64), jnp.float32)
        tbl_19 = 0.05 * jax.random.normal(jax.random.fold_in(_tk, 500 + 19), (125000, 64), jnp.float32)
        tbl_20 = 0.05 * jax.random.normal(jax.random.fold_in(_tk, 500 + 20), (12500, 64), jnp.float32)
        tbl_21 = 0.05 * jax.random.normal(jax.random.fold_in(_tk, 500 + 21), (12500, 64), jnp.float32)
        tbl_22 = 0.05 * jax.random.normal(jax.random.fold_in(_tk, 500 + 22), (1000, 64), jnp.float32)
        tbl_23 = 0.05 * jax.random.normal(jax.random.fold_in(_tk, 500 + 23), (1000, 64), jnp.float32)
        tbl_24 = 0.05 * jax.random.normal(jax.random.fold_in(_tk, 500 + 24), (12500, 64), jnp.float32)
        tbl_25 = 0.05 * jax.random.normal(jax.random.fold_in(_tk, 500 + 25), (1000, 64), jnp.float32)
        _rk = jax.random.fold_in(_tk, 7)
        r_dense_t = 7.22013e-05 + 1.00017 * jax.random.normal(jax.random.fold_in(_rk, 101), (512, 256), jnp.float32)
        W_top1 = 0.0360844 * jax.random.normal(jax.random.fold_in(_tk, 801), (768, 512), jnp.float32)
        W_top2 = 0.0441942 * jax.random.normal(jax.random.fold_in(_tk, 802), (512, 256), jnp.float32)
        W_top3 = 0.0625 * jax.random.normal(jax.random.fold_in(_tk, 803), (256, 1), jnp.float32)
        b_top1 = jnp.zeros((512,), jnp.float32)
        b_top2 = jnp.zeros((256,), jnp.float32)
        return (r_dense_t, ids, tbl_0, tbl_1, tbl_2, tbl_3, tbl_4, tbl_5, tbl_6, tbl_7, tbl_8, tbl_9, tbl_10, tbl_11, tbl_12, tbl_13, tbl_14, tbl_15, tbl_16, tbl_17, tbl_18, tbl_19, tbl_20, tbl_21, tbl_22, tbl_23, tbl_24, tbl_25, W_top1, b_top1, W_top2, b_top2, W_top3)
    r_dense_t, ids, tbl_0, tbl_1, tbl_2, tbl_3, tbl_4, tbl_5, tbl_6, tbl_7, tbl_8, tbl_9, tbl_10, tbl_11, tbl_12, tbl_13, tbl_14, tbl_15, tbl_16, tbl_17, tbl_18, tbl_19, tbl_20, tbl_21, tbl_22, tbl_23, tbl_24, tbl_25, W_top1, b_top1, W_top2, b_top2, W_top3 = _rec_inputs()

    def _L0_rec_setup():
        import jax, jax.numpy as jnp
        import numpy as np
        EPS = 1e-05
        NI = 33
        TRIL_I, TRIL_J = np.tril_indices(NI, k=-1)

        def layer_norm(x, g, b):
            m = jnp.mean(x, axis=-1, keepdims=True)
            v = jnp.mean(jnp.square(x - m), axis=-1, keepdims=True)
            return (x - m) * jax.lax.rsqrt(v + EPS) * g + b
        key = jax.random.key(seed)
        ks = jax.random.split(key, 8)
        B, D_DENSE, N_SP, D_SP = (4096, 256, 26, 64)
        E, PROJ, MAXD, NFLAT = (128, 32, 512, 528)
        dense_t = jax.random.normal(ks[0], (B, D_DENSE), dtype=jnp.float32)
        sparse_t = jax.random.normal(ks[1], (B, N_SP, D_SP), dtype=jnp.float32)
        Wd = jax.random.normal(ks[2], (E, D_DENSE), dtype=jnp.float32) / np.sqrt(D_DENSE)
        Ws = jax.random.normal(ks[3], (E, D_SP), dtype=jnp.float32) / np.sqrt(D_SP)
        Wsi = jax.random.normal(ks[4], (PROJ, N_SP), dtype=jnp.float32) / np.sqrt(N_SP)
        Wl = jax.random.normal(ks[5], (MAXD, NFLAT), dtype=jnp.float32) / np.sqrt(NFLAT)
        gd = jnp.ones((E,), jnp.float32)
        bd = jnp.zeros((E,), jnp.float32)
        gs = jnp.ones((E,), jnp.float32)
        bs = jnp.zeros((E,), jnp.float32)
        gsi = jnp.ones((PROJ,), jnp.float32)
        bsi = jnp.zeros((PROJ,), jnp.float32)
        gl = jnp.ones((MAXD,), jnp.float32)
        bl = jnp.zeros((MAXD,), jnp.float32)
        return {'dense_t': dense_t, 'sparse_t': sparse_t, 'Wd': Wd, 'gd': gd, 'bd': bd, 'Ws': Ws, 'gs': gs, 'bs': bs, 'Wsi': Wsi, 'gsi': gsi, 'bsi': bsi, 'Wl': Wl, 'gl': gl, 'bl': bl, 'dims_in_use': 384}
    _L0_rec_all = _L0_rec_setup()
    _L0_rec_in = {k: v for k, v in _L0_rec_all.items() if k in ('Wd', 'gd', 'bd', 'Ws', 'gs', 'bs', 'Wsi', 'gsi', 'bsi', 'Wl', 'gl', 'bl')}
    del _L0_rec_all
    return {'r_dense_t': r_dense_t, 'ids': ids, 'tbl_0': tbl_0, 'tbl_1': tbl_1, 'tbl_2': tbl_2, 'tbl_3': tbl_3, 'tbl_4': tbl_4, 'tbl_5': tbl_5, 'tbl_6': tbl_6, 'tbl_7': tbl_7, 'tbl_8': tbl_8, 'tbl_9': tbl_9, 'tbl_10': tbl_10, 'tbl_11': tbl_11, 'tbl_12': tbl_12, 'tbl_13': tbl_13, 'tbl_14': tbl_14, 'tbl_15': tbl_15, 'tbl_16': tbl_16, 'tbl_17': tbl_17, 'tbl_18': tbl_18, 'tbl_19': tbl_19, 'tbl_20': tbl_20, 'tbl_21': tbl_21, 'tbl_22': tbl_22, 'tbl_23': tbl_23, 'tbl_24': tbl_24, 'tbl_25': tbl_25, 'W_top1': W_top1, 'b_top1': b_top1, 'W_top2': W_top2, 'b_top2': b_top2, 'W_top3': W_top3, 'L0_rec_Wd': _L0_rec_in['Wd'], 'L0_rec_gd': _L0_rec_in['gd'], 'L0_rec_bd': _L0_rec_in['bd'], 'L0_rec_Ws': _L0_rec_in['Ws'], 'L0_rec_gs': _L0_rec_in['gs'], 'L0_rec_bs': _L0_rec_in['bs'], 'L0_rec_Wsi': _L0_rec_in['Wsi'], 'L0_rec_gsi': _L0_rec_in['gsi'], 'L0_rec_bsi': _L0_rec_in['bsi'], 'L0_rec_Wl': _L0_rec_in['Wl'], 'L0_rec_gl': _L0_rec_in['gl'], 'L0_rec_bl': _L0_rec_in['bl']}

def reference(r_dense_t, ids, tbl_0, tbl_1, tbl_2, tbl_3, tbl_4, tbl_5, tbl_6, tbl_7, tbl_8, tbl_9, tbl_10, tbl_11, tbl_12, tbl_13, tbl_14, tbl_15, tbl_16, tbl_17, tbl_18, tbl_19, tbl_20, tbl_21, tbl_22, tbl_23, tbl_24, tbl_25, W_top1, b_top1, W_top2, b_top2, W_top3, L0_rec_Wd, L0_rec_gd, L0_rec_bd, L0_rec_Ws, L0_rec_gs, L0_rec_bs, L0_rec_Wsi, L0_rec_gsi, L0_rec_bsi, L0_rec_Wl, L0_rec_gl, L0_rec_bl):
    import jax
    import jax.numpy as jnp

    def _L0_rec_ref(dense_t, sparse_t, Wd, gd, bd, Ws, gs, bs, Wsi, gsi, bsi, Wl, gl, bl, dims_in_use):
        import jax, jax.numpy as jnp
        import numpy as np
        EPS = 1e-05
        NI = 33
        TRIL_I, TRIL_J = np.tril_indices(NI, k=-1)

        def layer_norm(x, g, b):
            m = jnp.mean(x, axis=-1, keepdims=True)
            v = jnp.mean(jnp.square(x - m), axis=-1, keepdims=True)
            return (x - m) * jax.lax.rsqrt(v + EPS) * g + b
        x = layer_norm(dense_t @ Wd.T, gd, bd)
        y = layer_norm(jnp.einsum('bnd,ed->bne', sparse_t, Ws), gs, bs)
        y = jnp.einsum('bne,pn->bep', y, Wsi)
        y = layer_norm(y, gsi, bsi)
        y = jnp.swapaxes(y, 1, 2)
        T = jnp.concatenate([x[:, None, :], y], axis=1)
        Z = jnp.einsum('bnd,bmd->bnm', T, T)
        Zflat = Z[:, TRIL_I, TRIL_J]
        out = layer_norm(Zflat @ Wl.T, gl, bl)
        maxd = out.shape[-1]
        mask = (jnp.arange(maxd) < dims_in_use).astype(out.dtype)
        return out * mask
    e = jnp.stack([tbl_0[ids[:, 0]], tbl_1[ids[:, 1]], tbl_2[ids[:, 2]], tbl_3[ids[:, 3]], tbl_4[ids[:, 4]], tbl_5[ids[:, 5]], tbl_6[ids[:, 6]], tbl_7[ids[:, 7]], tbl_8[ids[:, 8]], tbl_9[ids[:, 9]], tbl_10[ids[:, 10]], tbl_11[ids[:, 11]], tbl_12[ids[:, 12]], tbl_13[ids[:, 13]], tbl_14[ids[:, 14]], tbl_15[ids[:, 15]], tbl_16[ids[:, 16]], tbl_17[ids[:, 17]], tbl_18[ids[:, 18]], tbl_19[ids[:, 19]], tbl_20[ids[:, 20]], tbl_21[ids[:, 21]], tbl_22[ids[:, 22]], tbl_23[ids[:, 23]], tbl_24[ids[:, 24]], tbl_25[ids[:, 25]]], axis=1)
    z = _L0_rec_ref(r_dense_t, e, L0_rec_Wd, L0_rec_gd, L0_rec_bd, L0_rec_Ws, L0_rec_gs, L0_rec_bs, L0_rec_Wsi, L0_rec_gsi, L0_rec_bsi, L0_rec_Wl, L0_rec_gl, L0_rec_bl, 384)
    z = z.reshape(z.shape[0], -1)
    h = jnp.concatenate([z, r_dense_t], axis=1)
    h = jnp.maximum(h @ W_top1 + b_top1, 0.0)
    h = jnp.maximum(h @ W_top2 + b_top2, 0.0)
    y = h @ W_top3
    return y

_drawn_inputs = setup_inputs


def setup_inputs(seed=0):
    import zlib

    import numpy as np

    out = dict(_drawn_inputs(seed))
    spreads = {'b_top1': (0.0, 0.1),
     'b_top2': (0.0, 0.1),
     'L0_rec_gd': (1.0, 0.6),
     'L0_rec_bd': (0.0, 0.8),
     'L0_rec_gs': (1.0, 0.6),
     'L0_rec_bs': (0.0, 0.1),
     'L0_rec_gsi': (1.0, 0.2),
     'L0_rec_bsi': (0.0, 0.1),
     'L0_rec_gl': (1.0, 0.2),
     'L0_rec_bl': (0.0, 0.1)}
    factors = {}
    for name, (base, spread) in spreads.items():
        noise = np.random.default_rng([zlib.crc32(name.encode()), seed]).standard_normal(out[name].shape)
        drawn = base * np.exp(spread * noise) if base else spread * noise
        out[name] = jnp.asarray(drawn.astype(out[name].dtype))
    for name, factor in factors.items():
        out[name] = (out[name] * factor).astype(out[name].dtype)
    return out
```

```python
import numpy as np
import concourse.bass as bass
from concourse import mybir
from contextlib import ExitStack

BATCH = 512
N_SP = 26
D_SP = 64
E = 128
PROJ = 32
D_DENSE = 256
MAXD = 512
DIMS = 384
H1, H2 = 512, 256
EPS = 1e-5
P = 128

TILES = BATCH // P
HALF = P // 2
GROUPS = HALF * N_SP // P
CHUNKS = 4
EX = HALF // CHUNKS
SLOTS = 2 * EX // 4
COLS = EX * PROJ
LAST_OF = [((EX * (m + 1)) * N_SP - 1) // P for m in range(CHUNKS)]
PAIRS = [list(range(0 if m == 0 else LAST_OF[m - 1] + 1, LAST_OF[m] + 1)) for m in range(CHUNKS)]
NEEDS = [list(range(EX * m * N_SP // P, LAST_OF[m] + 1)) for m in range(CHUNKS)]
FIRST_EX = [P * g // N_SP for g in range(GROUPS)]
SPAN = max((P * g + P - 1) // N_SP - FIRST_EX[g] + 1 for g in range(GROUPS))

PAIR_CHUNKS = PROJ // 2 * PROJ // P
EXTRA = 2 + 2 * PROJ
GRAM = 2 + PROJ
DUP = PROJ // 2
ZB = 2 + (GRAM + DUP) * PROJ


def feature_pairs():
    k = 1 + np.arange(PAIR_CHUNKS)[:, None, None] * 4 + np.arange(4)[None, :, None]
    first = np.broadcast_to(np.arange(PROJ)[None, None, :], (PAIR_CHUNKS, 4, PROJ))
    return first.reshape(PAIR_CHUNKS, P), ((first + k) % PROJ).reshape(PAIR_CHUNKS, P), \
        np.broadcast_to(k, first.shape).reshape(PAIR_CHUNKS, P)


def example_order():
    order = np.zeros(P, np.int64)
    for b in range(P):
        half, m, i = b // HALF, b % HALF // EX, b % EX
        order[32 * (i % 4) + SLOTS * m + (EX // 4) * half + i // 4] = b
    return order


def dlrm_tower(nc, table, ids, setup_a, setup_b, w_pairs, w_dense_token, w_top1, w_top2, dense, w_dense, out):
    F32, BF16, I32 = mybir.dt.float32, mybir.dt.bfloat16, mybir.dt.int32
    ALU, ACT, AX = mybir.AluOpType, mybir.ActivationFunctionType, mybir.AxisListType
    HT = H1 // P

    ctx = ExitStack()
    with ctx:
        def sb(name, shape, dt=F32):
            return ctx.enter_context(nc.sbuf_tensor(name, shape, dt))

        def bank(name, cols=512):
            return ctx.enter_context(nc.psum_tensor(name, [P, cols], F32))

        def sem(name):
            return ctx.enter_context(nc.semaphore(name))

        ids_sb = sb("ids_sb", [P, TILES + 1, 2 * GROUPS], I32)
        idx = sb("idx", [P, TILES, 2 * GROUPS], I32)
        rows = sb("rows", [P, GROUPS, 2, D_SP])
        A = sb("setup_a_sb", [P, setup_a.shape[1]])
        B = sb("setup_b_sb", [P, setup_b.shape[1]])
        a_at, b_at = [0], [0]

        def part(of, at, n):
            at[0] += n
            return of[:, at[0] - n:at[0]]

        ident = part(A, a_at, P)
        centre = part(A, a_at, P)
        same_half = part(A, a_at, P)
        ws2 = part(A, a_at, P)
        gs_row = part(A, a_at, E)
        wsi_rows = part(A, a_at, GROUPS * PROJ).rearrange("p (g q) -> p g q", g=GROUPS)
        own = part(A, a_at, GROUPS * SPAN).rearrange("p (g j) -> p g j", g=GROUPS)
        wsi_t = part(A, a_at, PROJ)[0:N_SP, :]
        bs_row = part(A, a_at, E)[0:9, :]
        pick = part(A, a_at, 6)[0:9, :]

        gd = part(B, b_at, 1)
        bd = part(B, b_at, 1)
        gl = part(B, b_at, 3)
        bl = part(B, b_at, 3)
        b1 = part(B, b_at, HT)
        b2 = part(B, b_at, H2 // P)
        w3 = part(B, b_at, H2 // P)
        gb = part(B, b_at, 4 * PAIR_CHUNKS).rearrange("p (w c) -> p w c", w=4)
        gb_x = part(B, b_at, 2)[0:PROJ, :]
        hot = part(B, b_at, 3 * PAIR_CHUNKS * EXTRA).rearrange("p (w c n) -> p w c n", w=3, c=PAIR_CHUNKS)
        hot_x = part(B, b_at, 2 * EXTRA)[0:PROJ, :].rearrange("p (w n) -> p w n", w=2)

        ones = sb("ones", [P, P])
        eps = sb("eps", [P, 1])
        quad = sb("quad", [P, P])
        wsc = sb("wsc", [P, P])
        ws_g = sb("ws_g", [P, E])
        proj = sb("proj", [P, GROUPS, SPAN, PROJ])
        shift_l = sb("shift_l", [9, E], BF16)
        shift_r = sb("shift_r", [9, EX, PROJ], BF16)
        wsi_c = sb("wsi_c", [N_SP, PROJ])
        small = sb("small", [P, 64])
        split = sb("split", [9, 4, P])
        split_h = sb("split_h", [9, 3, P], BF16)
        wp = sb("wp", [P, PAIR_CHUNKS, MAXD])
        wx = sb("wx", [PROJ, MAXD])
        wf = sb("wf", [EXTRA, MAXD])
        m_sel = sb("m_sel", [P, PAIR_CHUNKS, EXTRA])
        m_tmp = sb("m_tmp", [P, PAIR_CHUNKS, EXTRA])
        m_x = sb("m_x", [PROJ, EXTRA])
        w1 = sb("w1", [P, 5, H1])
        w2 = sb("w2", [P, HT, H2])
        bias1 = sb("bias1", [P, HT])
        dn = sb("dn", [P, 2, BATCH])
        wd = sb("wd", [P, 2, E])
        xt = sb("xt", [P, BATCH])
        x_sq = sb("x_sq", [P, BATCH])
        x_sum = sb("x_sum", [P, TILES])

        rows_t = sb("rows_t", [P, 4, P])
        prod = sb("prod", [P, 4, 2, D_SP])
        q_var = sb("q_var", [P, 4, 2])
        q_std = sb("q_std", [P, 4, 2])
        q_inv = sb("q_inv", [P, 4, 2])
        mix = sb("mix", [P, COLS])
        sq = sb("sq", [P, 2 * COLS])
        y_var = sb("y_var", [P, 2 * EX])
        y_std = sb("y_std", [P, 2 * EX])
        y_inv = sb("y_inv", [P, 2 * EX])
        tok = sb("tok", [P, 2 * EX, GRAM])
        grams = sb("grams", [P, GRAM, CHUNKS * SLOTS])
        zb = sb("zb", [P, ZB])
        zp = sb("zp", [P, PAIR_CHUNKS * P])
        zt = sb("zt", [P, PAIR_CHUNKS + 1, P])
        z_sq = sb("z_sq", [P, 4, P])
        z_std = sb("z_std", [P, P])
        z_inv = sb("z_inv", [P, P])
        zn = sb("zn", [P, 3, P])
        dn_t = sb("dn_t", [P, 2, P])
        h1 = sb("h1", [P, HT, P])
        h2 = sb("h2", [P, H2 // P, P])
        y_sb = sb("y_sb", [1, BATCH])

        p_rt = bank("p_rt")
        p_q = bank("p_q")
        p_mix = bank("p_mix")
        p_y = bank("p_y", 1024)
        p_g = bank("p_g")
        p_a = bank("p_a")
        p_b = bank("p_b")

        ids_in, a_in, b_in, wp_in, w1_in, w2_in, dn_in = map(sem, (
            "ids_in", "a_in", "b_in", "wp_in", "w1_in", "w2_in", "dn_in"))
        dve_step, idx_made, const_made = map(sem, ("dve_step", "idx_made", "const_made"))
        setup_mm, setup_dve, setup_act = map(sem, ("setup_mm", "setup_dve", "setup_act"))
        gathered = [sem(f"gathered{m}") for m in range(CHUNKS)]
        rt_done, rt_out, q_done, prod_done, q_red, q_rooted, q_inverted, rows_scaled = map(sem, (
            "rt_done", "rt_out", "q_done", "prod_done", "q_red", "q_rooted", "q_inverted", "rows_scaled"))
        mix_done, mix_out, y_done, y_squared, y_red, y_rooted, y_inverted, tok_made, x_put = map(sem, (
            "mix_done", "mix_out", "y_done", "y_squared", "y_red", "y_rooted", "y_inverted", "tok_made", "x_put"))
        gram_done, gram_out, zb_made, zt_done, zt_out, zc_done, z_squared, zvar_done, z_rooted, z_inverted, z_turned = map(sem, (
            "gram_done", "gram_out", "zb_made", "zt_done", "zt_out", "zc_done", "z_squared", "zvar_done",
            "z_rooted", "z_inverted", "z_turned"))
        z_normed, dn_put, h1_done, h1_out, h2_done, h2_out, out_done, out_put, stored = map(sem, (
            "z_normed", "dn_put", "h1_done", "h1_out", "h2_done", "h2_out", "out_done", "out_put", "stored"))

        block = ctx.enter_context(nc.Block())

        def n(t, m=0):
            return CHUNKS * t + m + 1

        def chunk_cols(g, m):
            lo = max(FIRST_EX[g], EX * m)
            hi = min((P * g + P - 1) // N_SP, EX * m + EX - 1) + 1
            return (lo - EX * m) * PROJ, (hi - EX * m) * PROJ, lo - FIRST_EX[g], hi - FIRST_EX[g]

        @block.sync
        def _(sp):
            sp.dma_start(ids_sb[:, :, :], ids).then_inc(ids_in, 16)
            sp.dma_start(A[:, :], setup_a).then_inc(a_in, 16)
            sp.dma_start(wd[:, :, :], w_dense).then_inc(dn_in, 16)
            sp.dma_start(dn[:, :, :], dense).then_inc(dn_in, 16)
            sp.dma_start(B[:, :], setup_b).then_inc(b_in, 16)
            sp.dma_start(wp[:, :, :], w_pairs).then_inc(wp_in, 16)
            sp.dma_start(wx[:, :], w_dense_token).then_inc(wp_in, 16)
            sp.dma_start(w1[:, :, :], w_top1).then_inc(w1_in, 16)
            sp.dma_start(w2[:, :, :], w_top2).then_inc(w2_in, 16)
            sp.wait_ge(out_put, TILES)
            sp.dma_start(out, y_sb[:, :]).then_inc(stored, 16)
            sp.wait_ge(stored, 16)

        @block.gpsimd
        def _(pool):
            pool.wait_ge(ids_in, 16)

            pool.tensor_tensor(idx[:, :, :], ids_sb[:, 0:TILES, :],
                               ids_sb[:, TILES:TILES + 1, :].broadcast_to([P, TILES, 2 * GROUPS]), ALU.add)\
                .then_inc(idx_made, 1)
            pool.wait_ge(idx_made, 1)
            for t in range(TILES):
                for m in range(CHUNKS):
                    if t:
                        pool.wait_ge(mix_done, n(t - 1, min(m + 1, CHUNKS - 1)))
                    for g in PAIRS[m]:
                        for half in range(2):
                            c = half * GROUPS + g
                            pool.indirect_dma_start(
                                out=rows[:, g, half, :], out_offset=None, in_=table,
                                in_offset=bass.IndirectOffsetOnAxis(ap=idx[:, t, c:c + 1], axis=0))\
                                .then_inc(gathered[m], 16)

        @block.tensor
        def _(pe):
            pe.wait_ge(const_made, 1)
            pe.wait_ge(a_in, 16)
            pe.matmul(p_rt[:, 0:P], centre, ws2, start=True, stop=True)
            pe.matmul(p_rt[:, P:2 * P], ws2, centre, start=True, stop=True).then_inc(setup_mm, 1)
            pe.wait_ge(setup_dve, 1)
            pe.matmul(p_q[0:9, 0:PROJ], ones[0:N_SP, 0:9], wsi_c[:, :], start=True, stop=True).then_inc(setup_mm, 1)
            pe.wait_ge(setup_dve, 2)
            pe.matmul(p_mix[:, 0:P], wsc[:, :], wsc[:, :], start=True, stop=True).then_inc(setup_mm, 1)
            pe.wait_ge(setup_dve, 3)
            for k in range(2):
                mm = pe.matmul(p_a[:, :], wd[:, k, :], dn[:, k, :], start=(k == 0), stop=(k == 1))
            mm.then_inc(setup_mm, 1)
            pe.wait_ge(setup_act, 1)
            pe.matmul(p_b[:, :], ones[:, :], x_sq[:, :], start=True, stop=True).then_inc(setup_mm, 1)
            pe.wait_ge(setup_dve, 4)
            for c in range(PAIR_CHUNKS):
                pe.matmul(p_g[0:EXTRA, :], m_sel[:, c, :], wp[:, c, :], start=(c == 0), stop=False)
            pe.matmul(p_g[0:EXTRA, :], m_x[:, :], wx[:, :], start=False, stop=True).then_inc(setup_mm, 1)
            pe.wait_ge(w1_in, 16)
            for h in range(HT):
                for k in range(3):
                    mm = pe.matmul(p_y[:, h:h + 1], w1[:, k, h * P:(h + 1) * P], bl[:, k:k + 1],
                                   start=(k == 0), stop=(k == 2))
            mm.then_inc(setup_mm, 1)
            pe.wait_ge(setup_dve, 5)
            for t in range(TILES):
                mm = pe.matmul(p_y[:, 512 + t:513 + t], xt[:, t * P:(t + 1) * P], ones[:, 0:1],
                               start=True, stop=True)
            mm.then_inc(setup_mm, 1)
            pe.wait_ge(setup_dve, 6)
            pe.wait_ge(w2_in, 16)

            def transpose_rows(t, m):
                pe.wait_ge(gathered[m], 32 * len(PAIRS[m]) * (t + 1))
                for i, g in enumerate(PAIRS[m]):
                    mm = pe.transpose(p_rt[:, i * P:(i + 1) * P], rows[:, g, :, :].rearrange("p h d -> p (h d)"), ident)
                mm.then_inc(rt_done, 1)

            def quad_rows(t, m):
                pe.wait_ge(rt_out, n(t, m))
                for i in range(len(PAIRS[m])):
                    mm = pe.matmul(p_q[:, i * P:(i + 1) * P], rows_t[:, i, :], quad[:, :], start=True, stop=True)
                mm.then_inc(q_done, 1)

            def mix_tables(t, m):
                pe.wait_ge(rows_scaled, n(t, m))
                for i, g in enumerate(NEEDS[m]):
                    lo, hi, j0, j1 = chunk_cols(g, m)
                    mm = pe.matmul(p_mix[:, lo:hi], rows[:, g, :, :].rearrange("p h d -> p (h d)"), proj[:, g, j0:j1, :],
                                   start=(i == 0), stop=(i == len(NEEDS[m]) - 1), skip_group_check=True)
                mm.then_inc(mix_done, 1)

            def widen(t, m):
                pe.wait_ge(mix_out, n(t, m))
                for half in range(2):
                    o = p_y[:, half * COLS:(half + 1) * COLS]
                    r = slice(half * D_SP, (half + 1) * D_SP)
                    pe.matmul(o, ws_g[r, :], mix[r, :], start=True, stop=False)
                    mm = pe.matmul(o, shift_l[:, :], shift_r[:, :, :], start=False, stop=True)
                mm.then_inc(y_done, 1)

            def token_products(t, m):
                pe.wait_ge(tok_made, n(t, m))
                pe.wait_ge(x_put, n(t, m))
                for b in range(2 * EX):
                    i, j, s = b % EX, b % 4, (EX // 4) * (b // EX) + b % EX // 4
                    mm = pe.matmul(p_g[32 * j:32 * j + 32, s * GRAM:(s + 1) * GRAM], tok[:, b, 2:GRAM],
                                   tok[:, b, :], start=True, stop=True)
                mm.then_inc(gram_done, 1)

            def turn_features(t):
                pe.wait_ge(zb_made, t + 1)
                pe.transpose(p_b[0:EXTRA, 0:P], zb[:, 0:EXTRA], ident)
                for c in range(PAIR_CHUNKS):
                    mm = pe.transpose(p_a[:, c * P:(c + 1) * P], zp[:, c * P:(c + 1) * P], ident)
                mm.then_inc(zt_done, 1)

            def interact(t):
                pe.wait_ge(zt_out, t + 1)
                for o in range(4):
                    for c in range(PAIR_CHUNKS):
                        pe.matmul(p_a[:, o * P:(o + 1) * P], wp[:, c, o * P:(o + 1) * P], zt[:, c, :],
                                  start=(c == 0), stop=False)
                    mm = pe.matmul(p_a[:, o * P:(o + 1) * P], wf[:, o * P:(o + 1) * P],
                                   zt[0:EXTRA, PAIR_CHUNKS, :], start=False, stop=True)
                mm.then_inc(zc_done, 1)

            def feature_variance(t):
                pe.wait_ge(z_squared, t + 1)
                for o in range(4):
                    mm = pe.matmul(p_b[:, 0:P], ones[:, :], z_sq[:, o, :], start=(o == 0), stop=(o == 3))
                mm.then_inc(zvar_done, 1)

            def top1(t):
                pe.wait_ge(z_normed, t + 1)
                pe.wait_ge(dn_put, t + 1)
                for h in range(HT):
                    for k in range(5):
                        mm = pe.matmul(p_a[:, h * P:(h + 1) * P], w1[:, k, h * P:(h + 1) * P],
                                       dn_t[:, k - 3, :] if k >= 3 else zn[:, k, :], start=(k == 0), stop=(k == 4))
                mm.then_inc(h1_done, 1)

            def top2(t):
                pe.wait_ge(h1_out, t + 1)
                for o in range(H2 // P):
                    for k in range(HT):
                        mm = pe.matmul(p_b[:, o * P:(o + 1) * P], w2[:, k, o * P:(o + 1) * P], h1[:, k, :],
                                       start=(k == 0), stop=(k == HT - 1))
                mm.then_inc(h2_done, 1)

            def top3(t):
                pe.wait_ge(h2_out, t + 1)
                for k in range(H2 // P):
                    mm = pe.matmul(p_a[0:1, 0:P], w3[:, k:k + 1], h2[:, k, :], start=(k == 0), stop=(k == 1))
                mm.then_inc(out_done, 1)

            def tile(t, new=True, old=True):
                for m in range(CHUNKS):
                    late = old and m <= 1
                    if m == 2 and old:
                        turn_features(t - 1)
                    if m == 3 and old:
                        feature_variance(t - 1)
                    if new:
                        transpose_rows(t, m)
                    if new and m > 0:
                        mix_tables(t, m - 1)
                    elif old and m == 0:
                        mix_tables(t - 1, CHUNKS - 1)
                    if m == 2 and old:
                        interact(t - 1)
                    if new:
                        quad_rows(t, m)
                    if m == 3 and old:
                        top1(t - 1)
                    if late:
                        token_products(t - 1, CHUNKS - 2 + m)
                    elif new and m >= 2:
                        token_products(t, m - 2)
                    if m == 3 and old:
                        top2(t - 1)
                    if old and m == 0:
                        widen(t - 1, CHUNKS - 1)
                    elif new and m > 0:
                        widen(t, m - 1)
                    if m == 3 and old:
                        top3(t - 1)

            tile(0, old=False)
            with pe.Fori(1, TILES) as t:
                tile(t)
            tile(TILES, new=False)

        @block.scalar
        def _(act):
            act.wait_ge(const_made, 1)
            act.wait_ge(setup_mm, 4)
            act.activation(x_sq[:, :], p_a[:, :], ACT.Square, scale=float(E) ** -0.5).then_inc(setup_act, 1)
            act.wait_ge(setup_mm, 5)
            act.activation(xt[:, :], p_b[:, :], ACT.Sqrt, bias=eps[:, 0:1]).then_inc(setup_act, 1)

            def rows_out(t, m):
                act.wait_ge(rt_done, n(t, m))
                w = len(PAIRS[m]) * P
                act.activation(rows_t[:, 0:len(PAIRS[m]), :], p_rt[:, 0:w], ACT.Copy).then_inc(rt_out, 1)

            def mix_move(t, m):
                act.wait_ge(mix_done, n(t, m))
                act.activation(mix[:, :], p_mix[:, :], ACT.Copy).then_inc(mix_out, 1)

            def row_root(t, m):
                act.wait_ge(q_red, n(t, m))
                k = len(PAIRS[m])
                act.activation(q_std[:, 0:k, :], q_var[:, 0:k, :], ACT.Sqrt, bias=eps[:, 0:1]).then_inc(q_rooted, 1)

            def gram_move(t, m, again):
                if again:
                    act.wait_ge(zb_made, t)
                act.wait_ge(gram_done, n(t, m))
                act.activation(grams[:, :, m * SLOTS:(m + 1) * SLOTS].rearrange("p c s -> p s c"),
                               p_g[:, 0:SLOTS * GRAM].rearrange("p (s c) -> p s c", c=GRAM),
                               ACT.Copy).then_inc(gram_out, 1)

            def put_dense_token(t, m, first):
                if not first:
                    act.wait_ge(gram_done, n(t, m) - 1)
                src = xt[:, bass.ds(t * P, P)].rearrange("p (j s) -> p s j", j=4)[:, m * SLOTS:(m + 1) * SLOTS, :]
                act.activation(tok[:, :, 0].rearrange("p (s j) -> p s j", j=4), src, ACT.Copy).then_inc(x_put, 1)

            def square(t, m):
                act.wait_ge(y_done, n(t, m))
                act.activation(sq[:, :], p_y[:, :], ACT.Square, scale=float(PROJ) ** -0.5).then_inc(y_squared, 1)

            def token_root(t, m):
                act.wait_ge(y_red, n(t, m))
                act.activation(y_std[:, :], y_var[:, :], ACT.Sqrt, bias=eps[:, 0:1]).then_inc(y_rooted, 1)

            def features_out(t):
                act.wait_ge(zt_done, t + 1)
                act.activation(zt[:, 0:PAIR_CHUNKS, :], p_a[:, :], ACT.Copy)
                act.activation(zt[0:EXTRA, PAIR_CHUNKS, :], p_b[0:EXTRA, 0:P], ACT.Copy).then_inc(zt_out, 1)

            def feature_squares(t):
                act.wait_ge(zc_done, t + 1)
                act.activation(z_sq[:, :, :], p_a[:, :], ACT.Square, scale=float(MAXD) ** -0.5).then_inc(z_squared, 1)

            def feature_root(t):
                act.wait_ge(zvar_done, t + 1)
                act.activation(z_std[:, :], p_b[:, 0:P], ACT.Sqrt, bias=eps[:, 0:1]).then_inc(z_rooted, 1)
                act.activation(dn_t[:, :, :], dn[:, :, bass.ds(t * P, P)], ACT.Copy).then_inc(dn_put, 1)

            def relu1(t):
                act.wait_ge(h1_done, t + 1)
                for h in range(HT):
                    i = act.activation(h1[:, h, :], p_a[:, h * P:(h + 1) * P], ACT.Relu, bias=bias1[:, h:h + 1])
                i.then_inc(h1_out, 1)

            def relu2(t):
                act.wait_ge(h2_done, t + 1)
                for o in range(H2 // P):
                    i = act.activation(h2[:, o, :], p_b[:, o * P:(o + 1) * P], ACT.Relu, bias=b2[:, o:o + 1])
                i.then_inc(h2_out, 1)

            def outputs(t):
                act.wait_ge(out_done, t + 1)
                act.activation(y_sb[:, bass.ds(t * P, P)], p_a[0:1, 0:P], ACT.Copy).then_inc(out_put, 1)

            act.wait_ge(setup_dve, 6)

            def tile(t, new=True, old=True):
                for m in range(CHUNKS):
                    u, v = (t, m - 1) if m else (t - 1, CHUNKS - 1)
                    if m == 2 and old:
                        features_out(t - 1)
                    if m == 3 and old:
                        feature_root(t - 1)
                    if new:
                        rows_out(t, m)
                    if (new and m) or (old and not m):
                        mix_move(u, v)
                    if m == 2 and old:
                        feature_squares(t - 1)
                    if new:
                        row_root(t, m)
                    if m == 3 and old:
                        relu1(t - 1)
                    if old and m <= 1:
                        gram_move(t - 1, CHUNKS - 2 + m, False)
                    elif new and m >= 2:
                        gram_move(t, m - 2, old and m == 2)
                    if m == 3 and old:
                        relu2(t - 1)
                    if (new and m) or (old and not m):
                        put_dense_token(u, v, not old and m == 1)
                        square(u, v)
                        token_root(u, v)
                    if m == 3 and old:
                        outputs(t - 1)

            tile(0, old=False)
            with act.Fori(1, TILES) as t:
                tile(t)
            tile(TILES, new=False)

        @block.vector
        def _(dve):
            steps = [0]

            def done(i):
                steps[0] += 1
                i.then_inc(dve_step, 1)
                dve.wait_ge(dve_step, steps[0])

            dve.memset(ones[:, :], 1.0)
            dve.memset(tok[:, :, 1], 1.0)
            dve.memset(zb[:, 1:2], 1.0)
            dve.memset(eps[:, :], EPS).then_inc(const_made, 1)
            dve.wait_ge(const_made, 1)
            dve.wait_ge(a_in, 16)
            mean_t, mean_r = small[0:N_SP, 0:1], small[:, 8:8 + GROUPS]
            done(dve.tensor_reduce(mean_t, wsi_t, AX.X, ALU.add))
            done(dve.tensor_scalar(mean_t, mean_t, 1.0 / PROJ, None, ALU.mult))
            dve.tensor_scalar(wsi_c[:, :], wsi_t, mean_t, None, ALU.subtract).then_inc(setup_dve, 1)
            dve.wait_ge(setup_mm, 1)
            dve.tensor_copy(wsc[:, :], p_rt[:, 0:P]).then_inc(setup_dve, 1)
            dve.tensor_tensor(ws_g[:, :], p_rt[:, P:2 * P], gs_row, ALU.mult)
            done(dve.tensor_reduce(mean_r, wsi_rows, AX.X, ALU.add))
            done(dve.tensor_scalar(mean_r, mean_r, 1.0 / PROJ, None, ALU.mult))
            done(dve.tensor_tensor(wsi_rows, wsi_rows, mean_r.unsqueeze(2).broadcast_to([P, GROUPS, PROJ]), ALU.subtract))
            for g in range(GROUPS):
                i = dve.tensor_tensor(proj[:, g, :, :], wsi_rows[:, g, :].unsqueeze(1).broadcast_to([P, SPAN, PROJ]),
                                      own[:, g, :].unsqueeze(2).broadcast_to([P, SPAN, PROJ]), ALU.mult)
            done(i)
            dve.wait_ge(setup_mm, 2)
            for src, w, at, dst in ((bs_row, E, 0, shift_l[:, :]), (p_q[0:9, 0:PROJ], PROJ, 3, None)):
                done(dve.tensor_copy(split[:, 0, 0:w], src))
                for k in range(3):
                    done(dve.tensor_copy(split_h[:, k, 0:w], split[:, 0, 0:w]))
                    done(dve.tensor_copy(split[:, k + 1, 0:w], split_h[:, k, 0:w]))
                    if k < 2:
                        done(dve.tensor_tensor(split[:, 0, 0:w], split[:, 0, 0:w], split[:, k + 1, 0:w], ALU.subtract))
                done(dve.tensor_scalar(split[:, 1, 0:w], split[:, 1, 0:w], pick[:, at:at + 1], None, ALU.mult))
                for k in (1, 2):
                    done(dve.scalar_tensor_tensor(out=split[:, 1, 0:w], in0=split[:, k + 1, 0:w],
                                                  scalar=pick[:, at + k:at + k + 1], in1=split[:, 1, 0:w],
                                                  op0=ALU.mult, op1=ALU.add))
                if dst is not None:
                    done(dve.tensor_copy(dst, split[:, 1, 0:w]))
                else:
                    done(dve.tensor_copy(shift_r[:, :, :], split[:, 1, 0:w].unsqueeze(1).broadcast_to([9, EX, PROJ])))
            dve.wait_ge(setup_mm, 3)
            done(dve.tensor_tensor(quad[:, :], p_mix[:, 0:P], same_half, ALU.mult))
            dve.wait_ge(dn_in, 32)
            mean_d = small[:, 24:26]
            done(dve.tensor_reduce(mean_d, wd[:, :, :], AX.X, ALU.add))
            done(dve.tensor_scalar(mean_d, mean_d, 1.0 / E, None, ALU.mult))
            dve.tensor_tensor(wd[:, :, :], wd[:, :, :], mean_d.unsqueeze(2).broadcast_to([P, 2, E]),
                              ALU.subtract).then_inc(setup_dve, 1)
            dve.wait_ge(b_in, 16)
            ac, ca, cc, aa = (small[:, 32 + 4 * k:36 + 4 * k] for k in range(4))
            dve.tensor_tensor(ac, gb[:, 0, :], gb[:, 3, :], ALU.mult)
            dve.tensor_tensor(ca, gb[:, 1, :], gb[:, 2, :], ALU.mult)
            dve.tensor_tensor(cc, gb[:, 2, :], gb[:, 3, :], ALU.mult)
            done(dve.tensor_tensor(aa, gb[:, 0, :], gb[:, 1, :], ALU.mult))
            wide = [P, PAIR_CHUNKS, EXTRA]
            done(dve.tensor_tensor(m_sel[:, :, :], hot[:, 0, :, :], ac.unsqueeze(2).broadcast_to(wide), ALU.mult))
            for w, s in ((1, ca), (2, cc)):
                done(dve.tensor_tensor(m_tmp[:, :, :], hot[:, w, :, :], s.unsqueeze(2).broadcast_to(wide), ALU.mult))
                done(dve.tensor_tensor(m_sel[:, :, :], m_sel[:, :, :], m_tmp[:, :, :], ALU.add))
            done(dve.tensor_scalar(m_x[:, :], hot_x[:, 0, :], gb_x[:, 0:1], None, ALU.mult))
            dve.wait_ge(wp_in, 32)
            dve.scalar_tensor_tensor(out=m_x[:, :], in0=hot_x[:, 1, :], scalar=gb_x[:, 1:2], in1=m_x[:, :],
                                     op0=ALU.mult, op1=ALU.add).then_inc(setup_dve, 1)
            dve.wait_ge(setup_act, 2)
            done(dve.reciprocal(xt[:, :], xt[:, :]))
            done(dve.tensor_tensor(xt[:, :], xt[:, :], p_a[:, :], ALU.mult))
            dve.tensor_scalar(xt[:, :], xt[:, :], gd, bd, ALU.mult, ALU.add).then_inc(setup_dve, 1)
            rs, ms = small[:, 0:PAIR_CHUNKS], small[:, 4:4 + PAIR_CHUNKS]
            dve.wait_ge(setup_mm, 6)
            done(dve.tensor_reduce(rs, wp[:, :, :], AX.X, ALU.add))
            done(dve.scalar_tensor_tensor(out=ms, in0=rs, scalar=1.0 / MAXD, in1=aa, op0=ALU.mult, op1=ALU.mult))
            for c in range(PAIR_CHUNKS):
                dve.tensor_scalar(wp[:, c, :], wp[:, c, :], aa[:, c:c + 1], ms[:, c:c + 1], ALU.mult, ALU.subtract)
            rx = small[0:EXTRA, 60:61]
            done(dve.tensor_reduce(rx, p_g[0:EXTRA, :], AX.X, ALU.add))
            done(dve.tensor_scalar(rx, rx, 1.0 / MAXD, None, ALU.mult))
            dve.tensor_scalar(wf[:, :], p_g[0:EXTRA, :], rx, None, ALU.subtract)
            dve.wait_ge(setup_mm, 8)
            dve.tensor_tensor(bias1[:, :], p_y[:, 0:HT], b1, ALU.add)
            dve.tensor_copy(x_sum[:, :], p_y[:, 512:512 + TILES])
            for k in range(3):
                i = dve.tensor_scalar(w1[:, k, :], w1[:, k, :], gl[:, k:k + 1], None, ALU.mult)
            i.then_inc(setup_dve, 1)

            def scale_rows(t, m):
                k, g0 = len(PAIRS[m]), PAIRS[m][0]
                here = rows[:, g0:g0 + k, :, :]
                dve.wait_ge(q_done, n(t, m))
                dve.tensor_tensor(prod[:, 0:k, :, :], p_q[:, 0:k * P].rearrange("p (g h d) -> p g h d", h=2, d=D_SP),
                                  here, ALU.mult).then_inc(prod_done, 1)
                dve.wait_ge(prod_done, n(t, m))
                dve.tensor_reduce(q_var[:, 0:k, :], prod[:, 0:k, :, :], AX.X, ALU.add).then_inc(q_red, 1)
                dve.wait_ge(q_rooted, n(t, m))
                dve.reciprocal(q_inv[:, 0:k, :], q_std[:, 0:k, :]).then_inc(q_inverted, 1)
                dve.wait_ge(q_inverted, n(t, m))
                dve.tensor_tensor(here, here, q_inv[:, 0:k, :].unsqueeze(3).broadcast_to([P, k, 2, D_SP]),
                                  ALU.mult).then_inc(rows_scaled, 1)

            def make_tokens(t, m, first):
                dve.wait_ge(y_squared, n(t, m))
                dve.tensor_reduce(y_var[:, :], sq[:, :].rearrange("p (b q) -> p b q", q=PROJ), AX.X, ALU.add)\
                    .then_inc(y_red, 1)
                dve.wait_ge(y_rooted, n(t, m))
                dve.reciprocal(y_inv[:, :], y_std[:, :]).then_inc(y_inverted, 1)
                dve.wait_ge(y_inverted, n(t, m))
                if not first:
                    dve.wait_ge(gram_done, n(t, m) - 1)
                dve.tensor_tensor(tok[:, :, 2:GRAM], p_y[:, :].rearrange("p (b q) -> p b q", q=PROJ),
                                  y_inv[:, :].unsqueeze(2).broadcast_to([P, 2 * EX, PROJ]), ALU.mult)\
                    .then_inc(tok_made, 1)

            def features(t, again):
                dve.wait_ge(gram_out, n(t, CHUNKS - 1))
                if again:
                    dve.wait_ge(zt_done, t)
                dve.transpose(zb[:, 2:2 + GRAM * PROJ], grams[:, :, :].rearrange("p c s -> p (c s)"))\
                    .then_inc(z_turned, 1)
                dve.wait_ge(z_turned, 2 * t + 1)
                dve.tensor_copy(zb[:, 0:1], x_sum[:, bass.ds(t, 1)])
                at = 2 + GRAM * PROJ
                dve.tensor_copy(zb[:, at:at + DUP * PROJ], zb[:, 2 + 2 * PROJ:2 + (2 + DUP) * PROJ])\
                    .then_inc(z_turned, 1)
                dve.wait_ge(z_turned, 2 * t + 2)
                base = zb[:, EXTRA + PROJ:EXTRA + PROJ + 1]
                diagonals = bass.AP(base.tensor, base.offset, [base.ap[0], [PROJ, PROJ // 2], [PROJ + 1, PROJ]])
                dve.tensor_copy(zp[:, :].rearrange("p (k q) -> p k q", q=PROJ), diagonals).then_inc(zb_made, 1)

            def normalise(t):
                dve.wait_ge(z_rooted, t + 1)
                dve.reciprocal(z_inv[:, :], z_std[:, :]).then_inc(z_inverted, 1)
                dve.wait_ge(z_inverted, t + 1)
                dve.tensor_tensor(zn[:, :, :], p_a[:, 0:DIMS].rearrange("p (k b) -> p k b", k=3),
                                  z_inv[:, :].unsqueeze(1).broadcast_to([P, 3, P]), ALU.mult).then_inc(z_normed, 1)

            def tile(t, new=True, old=True, first=False):
                for m in range(CHUNKS):
                    u, v = (t, m - 1) if m else (t - 1, CHUNKS - 1)
                    if m == 3 and old:
                        normalise(t - 1)
                    if new:
                        scale_rows(t, m)
                    if (new and m) or (old and not m):
                        make_tokens(u, v, not old and m == 1)
                    if m == 1 and old:
                        features(t - 1, not first)

            tile(0, old=False)
            tile(1, first=True)
            with dve.Fori(2, TILES) as t:
                tile(t)
            tile(TILES, new=False)


def kernel(**inputs):
    import concourse.bacc as bacc
    from concourse.bass_utils import run_bass_kernel_spmd

    x = {k: np.asarray(v) for k, v in inputs.items()}
    tables = [x[f"tbl_{k}"] for k in range(N_SP)]
    table = np.concatenate(tables, axis=0)
    starts = np.cumsum([0] + [t.shape[0] for t in tables[:-1]]).astype(np.int32)

    def cols(*parts):
        out = []
        for p in parts:
            p = np.asarray(p, np.float32).reshape(p.shape[0], -1)
            out.append(np.concatenate([p, np.zeros((P - p.shape[0], p.shape[1]), np.float32)]))
        return np.ascontiguousarray(np.concatenate(out, axis=1))

    def halves(v, k):
        return v.reshape(k, P).T

    flat = np.arange(GROUPS * P).reshape(GROUPS, P)
    of_table, of_example = flat % N_SP, flat // N_SP
    offsets = np.tile(starts[of_table].T, (1, 2))
    ids = x["ids"].reshape(TILES, 2 * GROUPS, P).transpose(2, 0, 1)
    ids = np.ascontiguousarray(np.concatenate([ids, offsets[:, None, :]], axis=1)).astype(np.int32)

    wsi, ws = x["L0_rec_Wsi"], x["L0_rec_Ws"]
    eye = np.eye(P, dtype=np.float32)
    half_of = np.arange(P) // D_SP
    own = (of_example.T[:, :, None] == np.array(FIRST_EX)[None, :, None] + np.arange(SPAN)).astype(np.float32)
    pick = np.zeros((9, 6), np.float32)
    for i in range(9):
        pick[i, i // 3] = pick[i, 3 + i % 3] = 1
    setup_a = cols(eye, eye - np.float32(1 / P), (half_of[:, None] == half_of) / np.float32(E),
                   np.concatenate([ws, ws], axis=1), np.broadcast_to(x["L0_rec_gs"], (P, E)),
                   wsi.T[of_table.T], own, wsi.T, np.broadcast_to(x["L0_rec_bs"], (9, E)), pick)

    first, second, k = feature_pairs()
    i, j = np.maximum(first, second) + 1, np.minimum(first, second) + 1
    twice = (k == PROJ // 2) & (first >= PROJ // 2)
    wl_t = x["L0_rec_Wl"].T
    w_pairs = wl_t[i * (i - 1) // 2 + j]
    w_pairs[twice] = 0
    w_pairs = np.ascontiguousarray(w_pairs.transpose(1, 0, 2))
    tok = np.arange(PROJ) + 1
    w_dense_token = np.ascontiguousarray(wl_t[tok * (tok - 1) // 2])

    gsi, bsi = x["L0_rec_gsi"], x["L0_rec_bsi"]
    gb = np.stack([gsi[first], gsi[second], bsi[first], bsi[second]]).transpose(2, 0, 1)
    hot = np.zeros((P, 3, PAIR_CHUNKS, EXTRA), np.float32)
    for c in range(PAIR_CHUNKS):
        hot[np.arange(P), 0, c, 2 + PROJ + first[c]] = 1
        hot[np.arange(P), 1, c, 2 + PROJ + second[c]] = 1
        hot[:, 2, c, 1] = E
    hot_x = np.zeros((PROJ, 2, EXTRA), np.float32)
    hot_x[np.arange(PROJ), 0, 2 + np.arange(PROJ)] = 1
    hot_x[:, 1, 0] = 1
    setup_b = cols(x["L0_rec_gd"][:, None], x["L0_rec_bd"][:, None], halves(x["L0_rec_gl"][:DIMS], 3),
                   halves(x["L0_rec_bl"][:DIMS], 3), halves(x["b_top1"], H1 // P), halves(x["b_top2"], H2 // P),
                   halves(x["W_top3"][:, 0], H2 // P), gb, np.stack([gsi, bsi], axis=1), hot, hot_x)

    w1 = x["W_top1"]
    w1 = np.concatenate([w1[:DIMS], w1[MAXD:]]).reshape(5, P, H1).transpose(1, 0, 2)
    w2 = x["W_top2"].reshape(H1 // P, P, H2).transpose(1, 0, 2)
    order = example_order()
    dense = x["r_dense_t"].reshape(TILES, P, D_DENSE)[:, order].reshape(BATCH, 2, P).transpose(2, 1, 0)
    w_dense = x["L0_rec_Wd"].reshape(E, 2, P).transpose(2, 1, 0)

    arrays = {"table": table, "ids": ids, "setup_a": setup_a, "setup_b": setup_b, "w_pairs": w_pairs,
              "w_dense_token": w_dense_token, "w_top1": w1, "w_top2": w2, "dense": dense, "w_dense": w_dense}
    arrays = {f"in_{k}": np.ascontiguousarray(v) for k, v in arrays.items()}
    nc = bacc.Bacc("TRN2", target_bir_lowering=False, num_devices=1)
    args = [nc.dram_tensor(k, v.shape, mybir.dt.from_np(v.dtype), kind="ExternalInput").ap()
            for k, v in arrays.items()]
    out = nc.dram_tensor("out_y", (1, BATCH), mybir.dt.float32, kind="ExternalOutput").ap()
    dlrm_tower(nc, *args, out)
    r = run_bass_kernel_spmd(nc, [arrays], core_ids=[0])
    y = r.results[0]["out_y"].reshape(TILES, P)
    got = np.zeros((TILES, P), np.float32)
    got[:, order] = y
    return got.reshape(BATCH, 1)
```

```python
import numpy as np
import concourse.bass as bass
from concourse import mybir
from contextlib import ExitStack

BATCH = 512
N_SP = 26
D_SP = 64
E = 128
PROJ = 32
D_DENSE = 256
MAXD = 512
DIMS = 384
H1, H2 = 512, 256
EPS = 1e-5
P = 128

TILES = BATCH // P
HALF = P // 2
GROUPS = HALF * N_SP // P
CHUNKS = 4
EX = HALF // CHUNKS
SLOTS = 2 * EX // 4
COLS = EX * PROJ
LAST_OF = [((EX * (m + 1)) * N_SP - 1) // P for m in range(CHUNKS)]
PAIRS = [list(range(0 if m == 0 else LAST_OF[m - 1] + 1, LAST_OF[m] + 1)) for m in range(CHUNKS)]
NEEDS = [list(range(EX * m * N_SP // P, LAST_OF[m] + 1)) for m in range(CHUNKS)]
FIRST_EX = [P * g // N_SP for g in range(GROUPS)]
SPAN = max((P * g + P - 1) // N_SP - FIRST_EX[g] + 1 for g in range(GROUPS))

PAIR_CHUNKS = PROJ // 2 * PROJ // P
EXTRA = 2 + 2 * PROJ
GRAM = 2 + PROJ
DUP = PROJ // 2
ZB = 2 + (GRAM + DUP) * PROJ


def feature_pairs():
    k = 1 + np.arange(PAIR_CHUNKS)[:, None, None] * 4 + np.arange(4)[None, :, None]
    first = np.broadcast_to(np.arange(PROJ)[None, None, :], (PAIR_CHUNKS, 4, PROJ))
    return first.reshape(PAIR_CHUNKS, P), ((first + k) % PROJ).reshape(PAIR_CHUNKS, P), \
        np.broadcast_to(k, first.shape).reshape(PAIR_CHUNKS, P)


def example_order():
    order = np.zeros(P, np.int64)
    for b in range(P):
        half, m, i = b // HALF, b % HALF // EX, b % EX
        order[32 * (i % 4) + SLOTS * m + (EX // 4) * half + i // 4] = b
    return order


def dlrm_tower(nc, table, ids, setup_a, setup_b, w_pairs, w_dense_token, w_top1, w_top2, dense, w_dense, out):
    F32, BF16, I32 = mybir.dt.float32, mybir.dt.bfloat16, mybir.dt.int32
    ALU, ACT, AX = mybir.AluOpType, mybir.ActivationFunctionType, mybir.AxisListType
    HT = H1 // P

    ctx = ExitStack()
    with ctx:
        def sb(name, shape, dt=F32):
            return ctx.enter_context(nc.sbuf_tensor(name, shape, dt))

        def bank(name, cols=512):
            return ctx.enter_context(nc.psum_tensor(name, [P, cols], F32))

        def sem(name):
            return ctx.enter_context(nc.semaphore(name))

        ids_sb = sb("ids_sb", [P, TILES + 1, 2 * GROUPS], I32)
        idx = sb("idx", [P, TILES, 2 * GROUPS], I32)
        rows = sb("rows", [P, GROUPS, 2, D_SP])
        A = sb("setup_a_sb", [P, setup_a.shape[1]])
        B = sb("setup_b_sb", [P, setup_b.shape[1]])
        a_at, b_at = [0], [0]

        def part(of, at, n):
            at[0] += n
            return of[:, at[0] - n:at[0]]

        ident = part(A, a_at, P)
        centre = part(A, a_at, P)
        same_half = part(A, a_at, P)
        ws2 = part(A, a_at, P)
        gs_row = part(A, a_at, E)
        wsi_rows = part(A, a_at, GROUPS * PROJ).rearrange("p (g q) -> p g q", g=GROUPS)
        own = part(A, a_at, GROUPS * SPAN).rearrange("p (g j) -> p g j", g=GROUPS)
        wsi_t = part(A, a_at, PROJ)[0:N_SP, :]
        bs_row = part(A, a_at, E)[0:9, :]
        pick = part(A, a_at, 6)[0:9, :]
        eps = part(A, a_at, 1)

        gd = part(B, b_at, 1)
        bd = part(B, b_at, 1)
        gl = part(B, b_at, 3)
        bl = part(B, b_at, 3)
        b1 = part(B, b_at, HT)
        b2 = part(B, b_at, H2 // P)
        w3 = part(B, b_at, H2 // P)
        gb = part(B, b_at, 4 * PAIR_CHUNKS).rearrange("p (w c) -> p w c", w=4)
        gb_x = part(B, b_at, 2)[0:PROJ, :]
        hot = part(B, b_at, 3 * PAIR_CHUNKS * EXTRA).rearrange("p (w c n) -> p w c n", w=3, c=PAIR_CHUNKS)
        hot_x = part(B, b_at, 2 * EXTRA)[0:PROJ, :].rearrange("p (w n) -> p w n", w=2)

        ones = sb("ones", [P, P])
        quad = sb("quad", [P, P])
        wsc = sb("wsc", [P, P])
        ws_g = sb("ws_g", [P, E])
        proj = sb("proj", [P, GROUPS, SPAN, PROJ])
        shift_l = sb("shift_l", [9, E], BF16)
        shift_r = sb("shift_r", [9, EX, PROJ], BF16)
        wsi_c = sb("wsi_c", [N_SP, PROJ])
        small = sb("small", [P, 64])
        split = sb("split", [9, 2, E + PROJ])
        split_h = sb("split_h", [9, 3, E + PROJ], BF16)
        wp = sb("wp", [P, PAIR_CHUNKS, MAXD])
        wx = sb("wx", [PROJ, MAXD])
        wf = sb("wf", [EXTRA, MAXD])
        m_sel = sb("m_sel", [P, PAIR_CHUNKS, EXTRA])
        m_tmp = sb("m_tmp", [P, PAIR_CHUNKS, EXTRA])
        m_x = sb("m_x", [PROJ, EXTRA])
        w1 = sb("w1", [P, 5, H1])
        w2 = sb("w2", [P, HT, H2])
        bias1 = sb("bias1", [P, HT])
        dn = sb("dn", [P, 2, BATCH])
        wd = sb("wd", [P, 2, E])
        xt = sb("xt", [P, BATCH])
        x_sq = sb("x_sq", [P, BATCH])
        x_std = sb("x_std", [P, BATCH])
        x_sum = sb("x_sum", [P, TILES])

        rows_t = sb("rows_t", [P, 4, P])
        prod = sb("prod", [P, 4, 2, D_SP])
        q_var = sb("q_var", [P, 4, 2])
        q_std = sb("q_std", [P, 4, 2])
        q_inv = sb("q_inv", [P, 4, 2])
        mix = sb("mix", [P, COLS])
        sq = sb("sq", [P, 2 * COLS])
        y_var = sb("y_var", [P, 2 * EX])
        y_std = sb("y_std", [P, 2 * EX])
        y_inv = sb("y_inv", [P, 2 * EX])
        tok = sb("tok", [P, 2, 2 * EX, GRAM])
        grams = sb("grams", [P, GRAM, CHUNKS * SLOTS])
        zb = sb("zb", [P, ZB])
        zp = sb("zp", [P, PAIR_CHUNKS * P])
        zt = sb("zt", [P, PAIR_CHUNKS + 1, P])
        z_sq = sb("z_sq", [P, 4, P])
        z_sum = sb("z_sum", [P, P])
        z_std = sb("z_std", [P, P])
        z_inv = sb("z_inv", [P, P])
        zn = sb("zn", [P, 3, P])
        dn_t = sb("dn_t", [P, 2, P])
        h1 = sb("h1", [P, HT, P])
        h2 = sb("h2", [P, H2 // P, P])
        y_sb = sb("y_sb", [1, BATCH])

        p_rt = bank("p_rt")
        p_q = bank("p_q")
        p_mix = bank("p_mix")
        p_y = bank("p_y", 1024)
        p_g = bank("p_g")
        p_a = bank("p_a")
        p_b = bank("p_b")

        def sems(*names):
            return [ctx.enter_context(nc.semaphore(name)) for name in names]

        ids_in, a_in, b_in, wp_in, w1_in, w2_in, dn_in = sems(
            "ids_in", "a_in", "b_in", "wp_in", "w1_in", "w2_in", "dn_in")
        ones_made, tok_ones_made, dve_step, idx_made = sems("ones_made", "tok_ones_made", "dve_step", "idx_made")
        ws_centred, col_sums, ws_ws, x_proj, x_var, x_squared, x_rooted, extra_done, sums_done = sems(
            "ws_centred", "col_sums", "ws_ws", "x_proj", "x_var", "x_squared", "x_rooted", "extra_done", "sums_done")
        wsi_ready, wsc_ready, quad_ready, wd_ready, proj_ready, shift_ready, select_ready, x_ready, wf_ready, \
            top_ready = sems("wsi_ready", "wsc_ready", "quad_ready", "wd_ready", "proj_ready", "shift_ready",
                             "select_ready", "x_ready", "wf_ready", "top_ready")
        gathered = sems(*[f"gathered{m}" for m in range(CHUNKS)])
        rt_done, rt_out, q_done, prod_done, q_red, q_rooted, q_inverted, rows_scaled, mix_done, mix_out = sems(
            "rt_done", "rt_out", "q_done", "prod_done", "q_red", "q_rooted", "q_inverted", "rows_scaled",
            "mix_done", "mix_out")
        y_done, y_squared, y_red, y_rooted, y_inverted, tok_made, x_put, gram_done, gram_out = sems(
            "y_done", "y_squared", "y_red", "y_rooted", "y_inverted", "tok_made", "x_put", "gram_done", "gram_out")
        z_turned, zb_made, zt_done, zt_out, zc_done, z_squared, z_summed, zvar_done, z_rooted, z_inverted = sems(
            "z_turned", "zb_made", "zt_done", "zt_out", "zc_done", "z_squared", "z_summed", "zvar_done",
            "z_rooted", "z_inverted")
        z_normed, dn_put, h1_done, h1_out, h2_done, h2_out, out_done, out_put, stored = sems(
            "z_normed", "dn_put", "h1_done", "h1_out", "h2_done", "h2_out", "out_done", "out_put", "stored")

        block = ctx.enter_context(nc.Block())

        def back(t, m, k):
            return (t, m - k) if k <= m else (t - 1, m - k + CHUNKS)

        def real(t, m=0):
            return not isinstance(t, int) or 0 <= t < TILES

        def n(t, m=0):
            return CHUNKS * t + m + 1

        def free_after(eng, sem, count):
            if not isinstance(count, int) or count > 0:
                eng.wait_ge(sem, count)

        def chunk_cols(g, m):
            lo = max(FIRST_EX[g], EX * m)
            hi = min((P * g + P - 1) // N_SP, EX * m + EX - 1) + 1
            return (lo - EX * m) * PROJ, (hi - EX * m) * PROJ, lo - FIRST_EX[g], hi - FIRST_EX[g]

        @block.sync
        def _(sp):
            sp.dma_start(ids_sb[:, :, :], ids).then_inc(ids_in, 16)
            sp.dma_start(A[:, :], setup_a).then_inc(a_in, 16)
            sp.dma_start(wd[:, :, :], w_dense).then_inc(dn_in, 16)
            sp.dma_start(dn[:, :, :], dense).then_inc(dn_in, 16)
            sp.dma_start(B[:, :], setup_b).then_inc(b_in, 16)
            sp.dma_start(wp[:, :, :], w_pairs).then_inc(wp_in, 16)
            sp.dma_start(wx[:, :], w_dense_token).then_inc(wp_in, 16)
            sp.dma_start(w1[:, :, :], w_top1).then_inc(w1_in, 16)
            sp.dma_start(w2[:, :, :], w_top2).then_inc(w2_in, 16)
            sp.wait_ge(out_put, TILES)
            sp.dma_start(out, y_sb[:, :]).then_inc(stored, 16)
            sp.wait_ge(stored, 16)

        @block.gpsimd
        def _(pool):
            pool.wait_ge(ids_in, 16)
            pool.tensor_tensor(idx[:, :, :], ids_sb[:, 0:TILES, :],
                               ids_sb[:, TILES:TILES + 1, :].broadcast_to([P, TILES, 2 * GROUPS]), ALU.add)\
                .then_inc(idx_made, 1)
            pool.wait_ge(idx_made, 1)
            for t in range(TILES):
                for m in range(CHUNKS):
                    if t:
                        pool.wait_ge(mix_done, n(t - 1, min(m + 1, CHUNKS - 1)))
                    for g in PAIRS[m]:
                        for half in range(2):
                            c = half * GROUPS + g
                            pool.indirect_dma_start(
                                out=rows[:, g, half, :], out_offset=None, in_=table,
                                in_offset=bass.IndirectOffsetOnAxis(ap=idx[:, t, c:c + 1], axis=0))\
                                .then_inc(gathered[m], 16)

        @block.tensor
        def _(pe):
            pe.wait_ge(ones_made, 1)
            pe.wait_ge(a_in, 16)
            pe.matmul(p_rt[:, 0:P], centre, ws2, start=True, stop=True)
            pe.matmul(p_rt[:, P:2 * P], ws2, centre, start=True, stop=True).then_inc(ws_centred, 1)
            pe.wait_ge(wsi_ready, 1)
            pe.matmul(p_q[0:9, 0:PROJ], ones[0:N_SP, 0:9], wsi_c[:, :], start=True, stop=True).then_inc(col_sums, 1)
            pe.wait_ge(wsc_ready, 1)
            pe.matmul(p_mix[:, 0:P], wsc[:, :], wsc[:, :], start=True, stop=True).then_inc(ws_ws, 1)
            pe.wait_ge(wd_ready, 1)
            pe.wait_ge(dn_in, 32)
            for k in range(2):
                mm = pe.matmul(p_a[:, :], wd[:, k, :], dn[:, k, :], start=(k == 0), stop=(k == 1))
            mm.then_inc(x_proj, 1)
            pe.wait_ge(x_squared, 1)
            pe.matmul(p_b[:, :], ones[:, :], x_sq[:, :], start=True, stop=True).then_inc(x_var, 1)
            pe.wait_ge(quad_ready, 1)
            pe.wait_ge(proj_ready, 1)

            def extra_weights():
                pe.wait_ge(select_ready, 1)
                pe.wait_ge(x_rooted, 1)
                for c in range(PAIR_CHUNKS):
                    pe.matmul(p_b[0:EXTRA, :], m_sel[:, c, :], wp[:, c, :], start=(c == 0), stop=False)
                pe.matmul(p_b[0:EXTRA, :], m_x[:, :], wx[:, :], start=False, stop=True).then_inc(extra_done, 1)

            def bias_and_sums():
                pe.wait_ge(wf_ready, 1)
                pe.wait_ge(w1_in, 16)
                for h in range(HT):
                    for k in range(3):
                        pe.matmul(p_b[:, h:h + 1], w1[:, k, h * P:(h + 1) * P], bl[:, k:k + 1],
                                  start=(k == 0), stop=(k == 2))
                pe.wait_ge(x_ready, TILES)
                for t in range(TILES):
                    mm = pe.matmul(p_b[:, HT + t:HT + t + 1], xt[:, t * P:(t + 1) * P], ones[:, 0:1],
                                   start=True, stop=True)
                mm.then_inc(sums_done, 1)

            def transpose_rows(t, m):
                pe.wait_ge(gathered[m], 32 * len(PAIRS[m]) * (t + 1))
                for i, g in enumerate(PAIRS[m]):
                    mm = pe.transpose(p_rt[:, i * P:(i + 1) * P],
                                      rows[:, g, :, :].rearrange("p h d -> p (h d)"), ident)
                mm.then_inc(rt_done, 1)

            def quad_rows(t, m):
                pe.wait_ge(rt_out, n(t, m))
                for i in range(len(PAIRS[m])):
                    mm = pe.matmul(p_q[:, i * P:(i + 1) * P], rows_t[:, i, :], quad[:, :], start=True, stop=True)
                mm.then_inc(q_done, 1)

            def mix_tables(t, m):
                pe.wait_ge(rows_scaled, n(t, m))
                for i, g in enumerate(NEEDS[m]):
                    lo, hi, j0, j1 = chunk_cols(g, m)
                    mm = pe.matmul(p_mix[:, lo:hi], rows[:, g, :, :].rearrange("p h d -> p (h d)"),
                                   proj[:, g, j0:j1, :], start=(i == 0), stop=(i == len(NEEDS[m]) - 1),
                                   skip_group_check=True)
                mm.then_inc(mix_done, 1)

            def widen(t, m):
                pe.wait_ge(mix_out, n(t, m))
                for half in range(2):
                    free_after(pe, tok_made, 2 * n(t, m) - 3 + half)
                    o = p_y[:, half * COLS:(half + 1) * COLS]
                    r = slice(half * D_SP, (half + 1) * D_SP)
                    pe.matmul(o, ws_g[r, :], mix[r, :], start=True, stop=False)
                    pe.matmul(o, shift_l[:, :], shift_r[:, :, :], start=False, stop=True).then_inc(y_done, 1)

            def token_products(t, m):
                pe.wait_ge(tok_made, 2 * n(t, m))
                pe.wait_ge(x_put, n(t, m))
                free_after(pe, gram_out, n(t, m) - 1)
                for b in range(2 * EX):
                    j, s = b % 4, (EX // 4) * (b // EX) + b % EX // 4
                    mm = pe.matmul(p_g[32 * j:32 * j + 32, s * GRAM:(s + 1) * GRAM], tok[:, m % 2, b, 2:GRAM],
                                   tok[:, m % 2, b, :], start=True, stop=True)
                mm.then_inc(gram_done, 1)

            def turn_features(t):
                pe.wait_ge(zb_made, t + 1)
                free_after(pe, out_put, t)
                pe.transpose(p_b[0:EXTRA, 0:P], zb[:, 0:EXTRA], ident)
                for c in range(PAIR_CHUNKS):
                    mm = pe.transpose(p_a[:, c * P:(c + 1) * P], zp[:, c * P:(c + 1) * P], ident)
                mm.then_inc(zt_done, 1)

            def interact(t):
                pe.wait_ge(zt_out, t + 1)
                for o in range(4):
                    for c in range(PAIR_CHUNKS):
                        pe.matmul(p_a[:, o * P:(o + 1) * P], wp[:, c, o * P:(o + 1) * P], zt[:, c, :],
                                  start=(c == 0), stop=False)
                    mm = pe.matmul(p_a[:, o * P:(o + 1) * P], wf[:, o * P:(o + 1) * P],
                                   zt[0:EXTRA, PAIR_CHUNKS, :], start=False, stop=True)
                mm.then_inc(zc_done, 1)

            def feature_variance(t):
                pe.wait_ge(z_summed, t + 1)
                pe.matmul(p_b[:, 0:P], ones[:, :], z_sum[:, :], start=True, stop=True).then_inc(zvar_done, 1)

            def top1(t):
                pe.wait_ge(z_normed, t + 1)
                pe.wait_ge(dn_put, t + 1)
                for h in range(HT):
                    for k in range(5):
                        mm = pe.matmul(p_a[:, h * P:(h + 1) * P], w1[:, k, h * P:(h + 1) * P],
                                       dn_t[:, k - 3, :] if k >= 3 else zn[:, k, :], start=(k == 0), stop=(k == 4))
                mm.then_inc(h1_done, 1)

            def top2(t):
                pe.wait_ge(h1_out, t + 1)
                for o in range(H2 // P):
                    for k in range(HT):
                        mm = pe.matmul(p_b[:, o * P:(o + 1) * P], w2[:, k, o * P:(o + 1) * P], h1[:, k, :],
                                       start=(k == 0), stop=(k == HT - 1))
                mm.then_inc(h2_done, 1)

            def top3(t):
                pe.wait_ge(h2_out, t + 1)
                for k in range(H2 // P):
                    mm = pe.matmul(p_a[0:1, 0:P], w3[:, k:k + 1], h2[:, k, :], start=(k == 0), stop=(k == 1))
                mm.then_inc(out_done, 1)

            def step(t, m):
                if m == 3 and real(t - 1):
                    turn_features(t - 1)
                if m == 0 and real(t - 2):
                    feature_variance(t - 2)
                if real(t):
                    transpose_rows(t, m)
                if m == 1 and real(t - 2):
                    top2(t - 2)
                before, third = back(t, m, 1), back(t, m, 3)
                if real(*before):
                    mix_tables(*before)
                if m == 3 and real(t - 1):
                    interact(t - 1)
                if real(t):
                    quad_rows(t, m)
                if m == 1 and real(t - 2):
                    top3(t - 2)
                if real(*third):
                    token_products(*third)
                if m == 0 and real(t - 2):
                    top1(t - 2)
                if real(*before):
                    widen(*before)

            for t in range(2):
                for m in range(CHUNKS):
                    if (t, m) == (0, 1):
                        pe.wait_ge(proj_ready, 2)
                        pe.wait_ge(shift_ready, 1)
                    step(t, m)
                    if (t, m) == (0, 2):
                        extra_weights()
                    if (t, m) == (0, 3):
                        bias_and_sums()
                    if (t, m) == (1, 2):
                        pe.wait_ge(top_ready, 1)
                        pe.wait_ge(w2_in, 16)
            with pe.Fori(2, TILES) as t:
                for m in range(CHUNKS):
                    step(t, m)
            for m in range(CHUNKS):
                step(TILES, m)
            for m in range(2):
                step(TILES + 1, m)

        @block.scalar
        def _(act):
            act.wait_ge(a_in, 16)
            act.activation(q_std[:, 0, 0:1], eps, ACT.Sqrt)
            act.wait_ge(x_proj, 1)
            act.activation(x_sq[:, :], p_a[:, :], ACT.Square, scale=float(E) ** -0.5).then_inc(x_squared, 1)
            act.wait_ge(x_var, 1)
            act.activation(x_std[:, :], p_b[:, :], ACT.Sqrt, bias=eps).then_inc(x_rooted, 1)

            def rows_out(t, m):
                act.wait_ge(rt_done, n(t, m))
                w = len(PAIRS[m]) * P
                act.activation(rows_t[:, 0:len(PAIRS[m]), :], p_rt[:, 0:w], ACT.Copy).then_inc(rt_out, 1)

            def mix_move(t, m):
                act.wait_ge(mix_done, n(t, m))
                act.activation(mix[:, :], p_mix[:, :], ACT.Copy).then_inc(mix_out, 1)

            def row_root(t, m):
                act.wait_ge(q_red, n(t, m))
                k = len(PAIRS[m])
                act.activation(q_std[:, 0:k, :], q_var[:, 0:k, :], ACT.Sqrt, bias=eps).then_inc(q_rooted, 1)

            def gram_move(t, m):
                if m == 0:
                    free_after(act, zb_made, t)
                act.wait_ge(gram_done, n(t, m))
                act.activation(grams[:, :, m * SLOTS:(m + 1) * SLOTS].rearrange("p c s -> p s c"),
                               p_g[:, 0:SLOTS * GRAM].rearrange("p (s c) -> p s c", c=GRAM),
                               ACT.Copy).then_inc(gram_out, 1)

            def put_dense_token(t, m):
                if isinstance(t, int):
                    act.wait_ge(x_ready, t + 1)
                src = xt[:, bass.ds(t * P, P)].rearrange("p (j s) -> p s j", j=4)[:, m * SLOTS:(m + 1) * SLOTS, :]
                act.activation(tok[:, m % 2, :, 0].rearrange("p (s j) -> p s j", j=4), src, ACT.Copy)\
                    .then_inc(x_put, 1)

            def square(t, m):
                for half in range(2):
                    act.wait_ge(y_done, 2 * n(t, m) - 1 + half)
                    act.activation(sq[:, half * COLS:(half + 1) * COLS], p_y[:, half * COLS:(half + 1) * COLS],
                                   ACT.Square, scale=float(PROJ) ** -0.5).then_inc(y_squared, 1)

            def token_root(t, m):
                act.wait_ge(y_red, 2 * n(t, m))
                act.activation(y_std[:, :], y_var[:, :], ACT.Sqrt, bias=eps).then_inc(y_rooted, 1)

            def features_out(t):
                act.wait_ge(zt_done, t + 1)
                act.activation(zt[:, 0:PAIR_CHUNKS, :], p_a[:, :], ACT.Copy)
                act.activation(zt[0:EXTRA, PAIR_CHUNKS, :], p_b[0:EXTRA, 0:P], ACT.Copy).then_inc(zt_out, 1)

            def feature_squares(t):
                act.wait_ge(zc_done, t + 1)
                act.activation(z_sq[:, :, :], p_a[:, :], ACT.Square, scale=float(MAXD) ** -0.5).then_inc(z_squared, 1)

            def feature_root(t):
                act.wait_ge(zvar_done, t + 1)
                act.activation(z_std[:, :], p_b[:, 0:P], ACT.Sqrt, bias=eps).then_inc(z_rooted, 1)
                act.activation(dn_t[:, :, :], dn[:, :, bass.ds(t * P, P)], ACT.Copy).then_inc(dn_put, 1)

            def relu1(t):
                act.wait_ge(h1_done, t + 1)
                for h in range(HT):
                    i = act.activation(h1[:, h, :], p_a[:, h * P:(h + 1) * P], ACT.Relu, bias=bias1[:, h:h + 1])
                i.then_inc(h1_out, 1)

            def relu2(t):
                act.wait_ge(h2_done, t + 1)
                for o in range(H2 // P):
                    i = act.activation(h2[:, o, :], p_b[:, o * P:(o + 1) * P], ACT.Relu, bias=b2[:, o:o + 1])
                i.then_inc(h2_out, 1)

            def outputs(t):
                act.wait_ge(out_done, t + 1)
                act.activation(y_sb[:, bass.ds(t * P, P)], p_a[0:1, 0:P], ACT.Copy).then_inc(out_put, 1)

            def step(t, m):
                before, second, third = (back(t, m, k) for k in (1, 2, 3))
                if m == 3 and real(t - 1):
                    features_out(t - 1)
                if m == 0 and real(t - 2):
                    feature_root(t - 2)
                if real(t):
                    rows_out(t, m)
                if real(*second):
                    token_root(*second)
                if m == 1 and real(t - 2):
                    relu2(t - 2)
                if real(*before):
                    mix_move(*before)
                if m == 3 and real(t - 1):
                    feature_squares(t - 1)
                if real(t):
                    row_root(t, m)
                if real(*third):
                    gram_move(*third)
                if m == 0 and real(t - 2):
                    relu1(t - 2)
                if m == 1 and real(t - 2):
                    outputs(t - 2)
                if real(*before):
                    put_dense_token(*before)
                    square(*before)

            for t in range(2):
                for m in range(CHUNKS):
                    step(t, m)
            act.wait_ge(top_ready, 1)
            with act.Fori(2, TILES) as t:
                for m in range(CHUNKS):
                    step(t, m)
            for m in range(CHUNKS):
                step(TILES, m)
            for m in range(2):
                step(TILES + 1, m)

        @block.vector
        def _(dve):
            steps = [0]

            def done(i):
                steps[0] += 1
                i.then_inc(dve_step, 1)
                dve.wait_ge(dve_step, steps[0])

            dve.memset(ones[:, :], 1.0).then_inc(ones_made, 1)
            dve.memset(tok[:, :, :, 1], 1.0)
            done(dve.memset(zb[:, 1:2], 1.0))
            dve.wait_ge(a_in, 16)
            mean_t, mean_r = small[0:N_SP, 0:1], small[:, 8:8 + GROUPS]
            done(dve.tensor_reduce(mean_t, wsi_t, AX.X, ALU.add))
            done(dve.tensor_scalar(mean_t, mean_t, 1.0 / PROJ, None, ALU.mult))
            dve.tensor_scalar(wsi_c[:, :], wsi_t, mean_t, None, ALU.subtract).then_inc(wsi_ready, 1)
            dve.wait_ge(ws_centred, 1)
            dve.tensor_copy(wsc[:, :], p_rt[:, 0:P]).then_inc(wsc_ready, 1)
            dve.tensor_tensor(ws_g[:, :], p_rt[:, P:2 * P], gs_row, ALU.mult)
            dve.wait_ge(dn_in, 32)
            mean_d = small[:, 24:26]
            done(dve.tensor_reduce(mean_d, wd[:, :, :], AX.X, ALU.add))
            done(dve.tensor_scalar(mean_d, mean_d, 1.0 / E, None, ALU.mult))
            dve.tensor_tensor(wd[:, :, :], wd[:, :, :], mean_d.unsqueeze(2).broadcast_to([P, 2, E]),
                              ALU.subtract).then_inc(wd_ready, 1)
            done(dve.tensor_reduce(mean_r, wsi_rows, AX.X, ALU.add))
            done(dve.tensor_scalar(mean_r, mean_r, 1.0 / PROJ, None, ALU.mult))
            done(dve.tensor_tensor(wsi_rows, wsi_rows, mean_r.unsqueeze(2).broadcast_to([P, GROUPS, PROJ]),
                                   ALU.subtract))

            def make_proj(g0, g1):
                wide = [P, g1 - g0, SPAN, PROJ]
                dve.tensor_tensor(proj[:, g0:g1, :, :], wsi_rows[:, g0:g1, :].unsqueeze(2).broadcast_to(wide),
                                  own[:, g0:g1, :].unsqueeze(3).broadcast_to(wide), ALU.mult).then_inc(proj_ready, 1)

            make_proj(0, LAST_OF[0] + 1)
            dve.wait_ge(col_sums, 1)
            dve.tensor_copy(split[:, 0, 0:E], bs_row)
            done(dve.tensor_copy(split[:, 0, E:E + PROJ], p_q[0:9, 0:PROJ]))
            dve.wait_ge(ws_ws, 1)
            dve.tensor_tensor(quad[:, :], p_mix[:, 0:P], same_half, ALU.mult).then_inc(quad_ready, 1)
            done(dve.tensor_copy(split_h[:, 0, :], split[:, 0, :]))
            done(dve.tensor_tensor(split[:, 1, :], split[:, 0, :], split_h[:, 0, :], ALU.subtract))
            done(dve.tensor_copy(split_h[:, 1, :], split[:, 1, :]))
            done(dve.tensor_tensor(split_h[:, 2, :], split[:, 1, :], split_h[:, 1, :], ALU.subtract))
            for lo, hi, at in ((0, E, 0), (E, E + PROJ, 3)):
                here = split[:, 0, lo:hi]
                done(dve.tensor_scalar(here, split_h[:, 0, lo:hi], pick[:, at:at + 1], None, ALU.mult))
                for k in (1, 2):
                    done(dve.scalar_tensor_tensor(out=here, in0=split_h[:, k, lo:hi],
                                                  scalar=pick[:, at + k:at + k + 1], in1=here,
                                                  op0=ALU.mult, op1=ALU.add))
            dve.tensor_copy(shift_l[:, :], split[:, 0, 0:E])
            dve.tensor_copy(shift_r[:, :, :], split[:, 0, E:E + PROJ].unsqueeze(1).broadcast_to([9, EX, PROJ]))\
                .then_inc(shift_ready, 1)

            def dense_token(t):
                at = slice(t * P, (t + 1) * P)
                dve.wait_ge(x_rooted, 1)
                done(dve.reciprocal(xt[:, at], x_std[:, at]))
                done(dve.tensor_tensor(xt[:, at], xt[:, at], p_a[:, at], ALU.mult))
                dve.tensor_scalar(xt[:, at], xt[:, at], gd, bd, ALU.mult, ALU.add).then_inc(x_ready, 1)

            ac, ca, cc, aa = (small[:, 32 + 4 * k:36 + 4 * k] for k in range(4))

            def selectors():
                dve.wait_ge(b_in, 16)
                dve.tensor_tensor(ac, gb[:, 0, :], gb[:, 3, :], ALU.mult)
                dve.tensor_tensor(ca, gb[:, 1, :], gb[:, 2, :], ALU.mult)
                dve.tensor_tensor(cc, gb[:, 2, :], gb[:, 3, :], ALU.mult)
                done(dve.tensor_tensor(aa, gb[:, 0, :], gb[:, 1, :], ALU.mult))
                wide = [P, PAIR_CHUNKS, EXTRA]
                done(dve.tensor_tensor(m_sel[:, :, :], hot[:, 0, :, :], ac.unsqueeze(2).broadcast_to(wide), ALU.mult))
                for w, s in ((1, ca), (2, cc)):
                    done(dve.tensor_tensor(m_tmp[:, :, :], hot[:, w, :, :], s.unsqueeze(2).broadcast_to(wide), ALU.mult))
                    done(dve.tensor_tensor(m_sel[:, :, :], m_sel[:, :, :], m_tmp[:, :, :], ALU.add))
                done(dve.tensor_scalar(m_x[:, :], hot_x[:, 0, :], gb_x[:, 0:1], None, ALU.mult))
                dve.wait_ge(wp_in, 32)
                dve.scalar_tensor_tensor(out=m_x[:, :], in0=hot_x[:, 1, :], scalar=gb_x[:, 1:2], in1=m_x[:, :],
                                         op0=ALU.mult, op1=ALU.add).then_inc(select_ready, 1)

            def pair_weights():
                rs, ms = small[:, 0:PAIR_CHUNKS], small[:, 4:4 + PAIR_CHUNKS]
                dve.wait_ge(extra_done, 1)
                for c in range(PAIR_CHUNKS):
                    i = dve.tensor_reduce(rs[:, c:c + 1], wp[:, c, :], AX.X, ALU.add)
                done(i)
                done(dve.scalar_tensor_tensor(out=ms, in0=rs, scalar=1.0 / MAXD, in1=aa, op0=ALU.mult, op1=ALU.mult))
                for c in range(PAIR_CHUNKS):
                    dve.tensor_scalar(wp[:, c, :], wp[:, c, :], aa[:, c:c + 1], ms[:, c:c + 1], ALU.mult, ALU.subtract)
                rx = small[0:EXTRA, 60:61]
                done(dve.tensor_reduce(rx, p_b[0:EXTRA, :], AX.X, ALU.add))
                done(dve.tensor_scalar(rx, rx, 1.0 / MAXD, None, ALU.mult))
                dve.tensor_scalar(wf[:, :], p_b[0:EXTRA, :], rx, None, ALU.subtract).then_inc(wf_ready, 1)

            def top_weights():
                dve.wait_ge(sums_done, 1)
                dve.tensor_tensor(bias1[:, :], p_b[:, 0:HT], b1, ALU.add)
                dve.tensor_copy(x_sum[:, :], p_b[:, HT:HT + TILES])
                for k in range(3):
                    i = dve.tensor_scalar(w1[:, k, :], w1[:, k, :], gl[:, k:k + 1], None, ALU.mult)
                i.then_inc(top_ready, 1)

            def scale_rows(t, m):
                k, g0 = len(PAIRS[m]), PAIRS[m][0]
                here = rows[:, g0:g0 + k, :, :]
                dve.wait_ge(q_done, n(t, m))
                dve.tensor_tensor(prod[:, 0:k, :, :], p_q[:, 0:k * P].rearrange("p (g h d) -> p g h d", h=2, d=D_SP),
                                  here, ALU.mult).then_inc(prod_done, 1)
                dve.wait_ge(prod_done, n(t, m))
                dve.tensor_reduce(q_var[:, 0:k, :], prod[:, 0:k, :, :], AX.X, ALU.add).then_inc(q_red, 1)
                dve.wait_ge(q_rooted, n(t, m))
                dve.reciprocal(q_inv[:, 0:k, :], q_std[:, 0:k, :]).then_inc(q_inverted, 1)
                dve.wait_ge(q_inverted, n(t, m))
                dve.tensor_tensor(here, here, q_inv[:, 0:k, :].unsqueeze(3).broadcast_to([P, k, 2, D_SP]),
                                  ALU.mult).then_inc(rows_scaled, 1)

            def token_variance(t, m):
                for half in range(2):
                    dve.wait_ge(y_squared, 2 * n(t, m) - 1 + half)
                    dve.tensor_reduce(y_var[:, half * EX:(half + 1) * EX],
                                      sq[:, half * COLS:(half + 1) * COLS].rearrange("p (b q) -> p b q", q=PROJ),
                                      AX.X, ALU.add).then_inc(y_red, 1)

            def make_tokens(t, m):
                dve.wait_ge(y_rooted, n(t, m))
                dve.reciprocal(y_inv[:, :], y_std[:, :]).then_inc(y_inverted, 1)
                dve.wait_ge(y_inverted, n(t, m))
                free_after(dve, gram_done, n(t, m) - 2)
                for half in range(2):
                    b = slice(half * EX, (half + 1) * EX)
                    dve.tensor_tensor(tok[:, m % 2, b, 2:GRAM],
                                      p_y[:, half * COLS:(half + 1) * COLS].rearrange("p (b q) -> p b q", q=PROJ),
                                      y_inv[:, b].unsqueeze(2).broadcast_to([P, EX, PROJ]), ALU.mult)\
                        .then_inc(tok_made, 1)

            def features(t):
                dve.wait_ge(gram_out, n(t, CHUNKS - 1))
                free_after(dve, zt_done, t)
                dve.transpose(zb[:, 2:2 + GRAM * PROJ], grams[:, :, :].rearrange("p c s -> p (c s)"))\
                    .then_inc(z_turned, 1)
                dve.wait_ge(z_turned, 2 * t + 1)
                dve.tensor_copy(zb[:, 0:1], x_sum[:, bass.ds(t, 1)])
                at = 2 + GRAM * PROJ
                dve.tensor_copy(zb[:, at:at + DUP * PROJ], zb[:, 2 + 2 * PROJ:2 + (2 + DUP) * PROJ])\
                    .then_inc(z_turned, 1)
                dve.wait_ge(z_turned, 2 * t + 2)
                base = zb[:, EXTRA + PROJ:EXTRA + PROJ + 1]
                diagonals = bass.AP(base.tensor, base.offset, [base.ap[0], [PROJ, PROJ // 2], [PROJ + 1, PROJ]])
                dve.tensor_copy(zp[:, :].rearrange("p (k q) -> p k q", q=PROJ), diagonals).then_inc(zb_made, 1)

            def sum_squares(t):
                dve.wait_ge(z_squared, t + 1)
                dve.tensor_reduce(z_sum[:, :], z_sq[:, :, :].rearrange("p o b -> p b o"), AX.X, ALU.add)\
                    .then_inc(z_summed, 1)

            def normalise(t):
                dve.wait_ge(z_rooted, t + 1)
                dve.reciprocal(z_inv[:, :], z_std[:, :]).then_inc(z_inverted, 1)
                dve.wait_ge(z_inverted, t + 1)
                free_after(dve, h1_done, t)
                dve.tensor_tensor(zn[:, :, :], p_a[:, 0:DIMS].rearrange("p (k b) -> p k b", k=3),
                                  z_inv[:, :].unsqueeze(1).broadcast_to([P, 3, P]), ALU.mult).then_inc(z_normed, 1)

            def step(t, m):
                before, second = (back(t, m, k) for k in (1, 2))
                if real(*second):
                    make_tokens(*second)
                if m == 0 and real(t - 2):
                    normalise(t - 2)
                if m == 3 and real(t - 1):
                    sum_squares(t - 1)
                if real(t):
                    scale_rows(t, m)
                if m == 2 and real(t - 1):
                    features(t - 1)
                if real(*before):
                    token_variance(*before)

            dve.wait_ge(b_in, 16)
            dense_token(0)
            step(0, 0)
            make_proj(LAST_OF[0] + 1, GROUPS)
            step(0, 1)
            selectors()
            dense_token(1)
            step(0, 2)
            dense_token(2)
            dense_token(3)
            step(0, 3)
            pair_weights()
            step(1, 0)
            top_weights()
            for m in range(1, CHUNKS):
                step(1, m)
            with dve.Fori(2, TILES) as t:
                for m in range(CHUNKS):
                    step(t, m)
            for m in range(CHUNKS):
                step(TILES, m)
            step(TILES + 1, 0)


def kernel(**inputs):
    import concourse.bacc as bacc
    from concourse.bass_utils import run_bass_kernel_spmd

    x = {k: np.asarray(v) for k, v in inputs.items()}
    tables = [x[f"tbl_{k}"] for k in range(N_SP)]
    table = np.concatenate(tables, axis=0)
    starts = np.cumsum([0] + [t.shape[0] for t in tables[:-1]]).astype(np.int32)

    def cols(*parts):
        out = []
        for p in parts:
            p = np.asarray(p, np.float32).reshape(p.shape[0], -1)
            out.append(np.concatenate([p, np.zeros((P - p.shape[0], p.shape[1]), np.float32)]))
        return np.ascontiguousarray(np.concatenate(out, axis=1))

    def halves(v, k):
        return v.reshape(k, P).T

    flat = np.arange(GROUPS * P).reshape(GROUPS, P)
    of_table, of_example = flat % N_SP, flat // N_SP
    offsets = np.tile(starts[of_table].T, (1, 2))
    ids = x["ids"].reshape(TILES, 2 * GROUPS, P).transpose(2, 0, 1)
    ids = np.ascontiguousarray(np.concatenate([ids, offsets[:, None, :]], axis=1)).astype(np.int32)

    wsi, ws = x["L0_rec_Wsi"], x["L0_rec_Ws"]
    eye = np.eye(P, dtype=np.float32)
    half_of = np.arange(P) // D_SP
    own = (of_example.T[:, :, None] == np.array(FIRST_EX)[None, :, None] + np.arange(SPAN)).astype(np.float32)
    pick = np.zeros((9, 6), np.float32)
    for i in range(9):
        pick[i, i // 3] = pick[i, 3 + i % 3] = 1
    setup_a = cols(eye, eye - np.float32(1 / P), (half_of[:, None] == half_of) / np.float32(E),
                   np.concatenate([ws, ws], axis=1), np.broadcast_to(x["L0_rec_gs"], (P, E)),
                   wsi.T[of_table.T], own, wsi.T, np.broadcast_to(x["L0_rec_bs"], (9, E)), pick,
                   np.full((P, 1), EPS, np.float32))

    first, second, k = feature_pairs()
    i, j = np.maximum(first, second) + 1, np.minimum(first, second) + 1
    twice = (k == PROJ // 2) & (first >= PROJ // 2)
    wl_t = x["L0_rec_Wl"].T
    w_pairs = wl_t[i * (i - 1) // 2 + j]
    w_pairs[twice] = 0
    w_pairs = np.ascontiguousarray(w_pairs.transpose(1, 0, 2))
    tok = np.arange(PROJ) + 1
    w_dense_token = np.ascontiguousarray(wl_t[tok * (tok - 1) // 2])

    gsi, bsi = x["L0_rec_gsi"], x["L0_rec_bsi"]
    gb = np.stack([gsi[first], gsi[second], bsi[first], bsi[second]]).transpose(2, 0, 1)
    hot = np.zeros((P, 3, PAIR_CHUNKS, EXTRA), np.float32)
    for c in range(PAIR_CHUNKS):
        hot[np.arange(P), 0, c, 2 + PROJ + first[c]] = 1
        hot[np.arange(P), 1, c, 2 + PROJ + second[c]] = 1
        hot[:, 2, c, 1] = E
    hot_x = np.zeros((PROJ, 2, EXTRA), np.float32)
    hot_x[np.arange(PROJ), 0, 2 + np.arange(PROJ)] = 1
    hot_x[:, 1, 0] = 1
    setup_b = cols(x["L0_rec_gd"][:, None], x["L0_rec_bd"][:, None], halves(x["L0_rec_gl"][:DIMS], 3),
                   halves(x["L0_rec_bl"][:DIMS], 3), halves(x["b_top1"], H1 // P), halves(x["b_top2"], H2 // P),
                   halves(x["W_top3"][:, 0], H2 // P), gb, np.stack([gsi, bsi], axis=1), hot, hot_x)

    w1 = x["W_top1"]
    w1 = np.concatenate([w1[:DIMS], w1[MAXD:]]).reshape(5, P, H1).transpose(1, 0, 2)
    w2 = x["W_top2"].reshape(H1 // P, P, H2).transpose(1, 0, 2)
    order = example_order()
    dense = x["r_dense_t"].reshape(TILES, P, D_DENSE)[:, order].reshape(BATCH, 2, P).transpose(2, 1, 0)
    w_dense = x["L0_rec_Wd"].reshape(E, 2, P).transpose(2, 1, 0)

    arrays = {"table": table, "ids": ids, "setup_a": setup_a, "setup_b": setup_b, "w_pairs": w_pairs,
              "w_dense_token": w_dense_token, "w_top1": w1, "w_top2": w2, "dense": dense, "w_dense": w_dense}
    arrays = {f"in_{k}": np.ascontiguousarray(v) for k, v in arrays.items()}
    nc = bacc.Bacc("TRN2", target_bir_lowering=False, num_devices=1)
    args = [nc.dram_tensor(k, v.shape, mybir.dt.from_np(v.dtype), kind="ExternalInput").ap()
            for k, v in arrays.items()]
    out = nc.dram_tensor("out_y", (1, BATCH), mybir.dt.float32, kind="ExternalOutput").ap()
    dlrm_tower(nc, *args, out)
    r = run_bass_kernel_spmd(nc, [arrays], core_ids=[0])
    y = r.results[0]["out_y"].reshape(TILES, P)
    got = np.zeros((TILES, P), np.float32)
    got[:, order] = y
    return got.reshape(BATCH, 1)
```

```python
import numpy as np
import concourse.bass as bass
from concourse import mybir
from contextlib import ExitStack

BATCH = 512
N_SP = 26
D_SP = 64
E = 128
PROJ = 32
D_DENSE = 256
MAXD = 512
DIMS = 384
H1, H2 = 512, 256
EPS = 1e-5
P = 128

TILES = BATCH // P
HALF = P // 2
GROUPS = HALF * N_SP // P
CHUNKS = 4
EX = HALF // CHUNKS
SLOTS = 2 * EX // 4
COLS = EX * PROJ
LAST_OF = [((EX * (m + 1)) * N_SP - 1) // P for m in range(CHUNKS)]
PAIRS = [list(range(0 if m == 0 else LAST_OF[m - 1] + 1, LAST_OF[m] + 1)) for m in range(CHUNKS)]
NEEDS = [list(range(EX * m * N_SP // P, LAST_OF[m] + 1)) for m in range(CHUNKS)]
FIRST_EX = [P * g // N_SP for g in range(GROUPS)]
SPAN = max((P * g + P - 1) // N_SP - FIRST_EX[g] + 1 for g in range(GROUPS))

PAIR_CHUNKS = PROJ // 2 * PROJ // P
EXTRA = 2 + 2 * PROJ
GRAM = 2 + PROJ
DUP = PROJ // 2
ZB = 2 + (GRAM + DUP) * PROJ


def feature_pairs():
    k = 1 + np.arange(PAIR_CHUNKS)[:, None, None] * 4 + np.arange(4)[None, :, None]
    first = np.broadcast_to(np.arange(PROJ)[None, None, :], (PAIR_CHUNKS, 4, PROJ))
    return first.reshape(PAIR_CHUNKS, P), ((first + k) % PROJ).reshape(PAIR_CHUNKS, P), \
        np.broadcast_to(k, first.shape).reshape(PAIR_CHUNKS, P)


def example_order():
    order = np.zeros(P, np.int64)
    for b in range(P):
        half, m, i = b // HALF, b % HALF // EX, b % EX
        order[32 * (i % 4) + SLOTS * m + (EX // 4) * half + i // 4] = b
    return order


def dlrm_tower(nc, table, ids, first, setup_a, setup_b, w_pairs, w_dense_token, w_top1, w_top1_dense, w_top2,
               dense, w_dense, out):
    F32, I32 = mybir.dt.float32, mybir.dt.int32
    ALU, ACT, AX = mybir.AluOpType, mybir.ActivationFunctionType, mybir.AxisListType
    HT = H1 // P

    ctx = ExitStack()
    with ctx:
        def sb(name, shape, dt=F32):
            return ctx.enter_context(nc.sbuf_tensor(name, shape, dt))

        def bank(name, cols=512):
            return ctx.enter_context(nc.psum_tensor(name, [P, cols], F32))

        ids_sb = sb("ids_sb", [P, TILES + 1, 2 * GROUPS], I32)
        idx = sb("idx", [P, TILES, 2 * GROUPS], I32)
        rows = sb("rows", [P, GROUPS, 2, D_SP])
        F = sb("first_sb", [P, first.shape[1]])
        A = sb("setup_a_sb", [P, setup_a.shape[1]])
        B = sb("setup_b_sb", [P, setup_b.shape[1]])
        f_at, a_at, b_at = [0], [0], [0]

        def part(of, at, n):
            at[0] += n
            return of[:, at[0] - n:at[0]]

        centre = part(F, f_at, P)
        ws2 = part(F, f_at, P)
        wsi_t = part(F, f_at, PROJ)[0:N_SP, :]
        eps = part(F, f_at, 1)

        ident = part(A, a_at, P)
        same_half = part(A, a_at, P)
        gs_row = part(A, a_at, E)
        wsi_rows = part(A, a_at, GROUPS * PROJ).rearrange("p (g q) -> p g q", g=GROUPS)
        own = part(A, a_at, GROUPS * SPAN).rearrange("p (g j) -> p g j", g=GROUPS)
        bs_row = part(A, a_at, E)[D_SP:D_SP + 1, :]

        gd = part(B, b_at, 1)
        bd = part(B, b_at, 1)
        gl = part(B, b_at, 3)
        bl = part(B, b_at, 3)
        b1 = part(B, b_at, HT)
        b2 = part(B, b_at, H2 // P)
        w3 = part(B, b_at, H2 // P)
        gb = part(B, b_at, 4 * PAIR_CHUNKS).rearrange("p (w c) -> p w c", w=4)
        gb_x = part(B, b_at, 2)[0:PROJ, :]
        hot = part(B, b_at, 3 * PAIR_CHUNKS * EXTRA).rearrange("p (w c n) -> p w c n", w=3, c=PAIR_CHUNKS)
        hot_x = part(B, b_at, 2 * EXTRA)[0:PROJ, :].rearrange("p (w n) -> p w n", w=2)

        ones = sb("ones", [P, P])
        quad = sb("quad", [P, P])
        wsc = sb("wsc", [P, P])
        ws_g = sb("ws_g", [D_SP + 1, E])
        proj = sb("proj", [P, GROUPS, SPAN, PROJ])
        wsi_c = sb("wsi_c", [N_SP, PROJ])
        small = sb("small", [P, 64])
        ac, ca, cc, aa = (small[:, 32 + 4 * k:36 + 4 * k] for k in range(4))
        row_sum, less_mean = small[:, 48:52], small[:, 52:56]
        row_sum_x, less_mean_x = small[0:EXTRA, 56:57], small[0:EXTRA, 57:58]
        wp = sb("wp", [P, PAIR_CHUNKS, MAXD])
        wx = sb("wx", [PROJ, MAXD])
        wf = sb("wf", [EXTRA, MAXD])
        m_sel = sb("m_sel", [P, PAIR_CHUNKS, EXTRA])
        m_tmp = sb("m_tmp", [P, PAIR_CHUNKS, EXTRA])
        m_x = sb("m_x", [PROJ, EXTRA])
        w1 = sb("w1", [P, 3, H1])
        w1_d = sb("w1_d", [P, 2, H1])
        w2 = sb("w2", [P, HT, H2])
        bias1 = sb("bias1", [P, HT])
        bias_row = sb("bias_row", [1, H1])
        dn = sb("dn", [P, 2, BATCH])
        wd = sb("wd", [P, 2, E])
        xt = sb("xt", [P, BATCH])
        x_sq = sb("x_sq", [P, BATCH])
        x_std = sb("x_std", [P, BATCH])
        h1_dense = sb("h1_dense", [P, HT, BATCH])

        rows_t = sb("rows_t", [P, 4, P])
        prod = sb("prod", [P, 4, 2, D_SP])
        q_var = sb("q_var", [P, 4, 2])
        q_std = sb("q_std", [P, 4, 2])
        q_inv = sb("q_inv", [P, 4, 2])
        mix = sb("mix", [D_SP + 1, 2, EX, PROJ])
        sq = sb("sq", [P, 2 * COLS])
        y_var = sb("y_var", [P, 2 * EX])
        y_std = sb("y_std", [P, 2 * EX])
        y_inv = sb("y_inv", [P, 2 * EX])
        tok = sb("tok", [P, 2, 2 * EX, GRAM])
        grams = sb("grams", [P, GRAM, CHUNKS * SLOTS])
        zb = sb("zb", [P, ZB])
        zp = sb("zp", [P, PAIR_CHUNKS * P])
        zt = sb("zt", [P, PAIR_CHUNKS + 1, P])
        zc_loop = sb("zc", [P, 4, P])
        zc_last = sb("zc_last", [P, 4, P])
        z_sq = sb("z_sq", [P, 4, P])
        z_sum = sb("z_sum", [P, P])
        z_std = sb("z_std", [P, P])
        z_inv = sb("z_inv", [P, P])
        h1_pre = sb("h1_pre", [P, HT, P])
        h1_loop = sb("h1", [P, HT, P])
        h1_last = sb("h1_last", [P, HT, P])
        h2 = sb("h2", [P, H2 // P, P])
        y_sb = sb("y_sb", [1, BATCH])

        p_rt = bank("p_rt")
        p_q = bank("p_q")
        p_mix = bank("p_mix")
        p_y = bank("p_y", 1024)
        p_g = bank("p_g")
        p_a = bank("p_a")
        p_b = bank("p_b")

        def sems(*names):
            return [ctx.enter_context(nc.semaphore(name)) for name in names]

        ids_in, first_in, a_in, b_in, wp_in, w1_in, w1_d_in, w2_in, wd_in, dn_in = sems(
            "ids_in", "first_in", "a_in", "b_in", "wp_in", "w1_in", "w1_d_in", "w2_in", "wd_in", "dn_in")
        ones_made, dve_step, idx_made = sems("ones_made", "dve_step", "idx_made")
        ws_centred, col_sums, ws_ws, x_proj, x_var, x_squared, x_rooted, extra_done, bias_done = sems(
            "ws_centred", "col_sums", "ws_ws", "x_proj", "x_var", "x_squared", "x_rooted", "extra_done",
            "bias_done")
        wsi_ready, wsc_ready, quad_ready, wd_ready, proj_ready, bs_ready, select_ready, x_ready = sems(
            "wsi_ready", "wsc_ready", "quad_ready", "wd_ready", "proj_ready", "bs_ready", "select_ready", "x_ready")
        dense_done, dense_out, pair_means, extra_mean, pairs_ready, wf_ready, bias_ready, top_ready = sems(
            "dense_done", "dense_out", "pair_means", "extra_mean", "pairs_ready", "wf_ready", "bias_ready", "top_ready")
        bias_out, bias_turned, share_ready = sems("bias_out", "bias_turned", "share_ready")
        gathered = sems(*[f"gathered{m}" for m in range(CHUNKS)])
        rt_done, rt_out, q_done, prod_done, q_red, q_rooted, q_inverted, rows_scaled, mix_done, mix_out = sems(
            "rt_done", "rt_out", "q_done", "prod_done", "q_red", "q_rooted", "q_inverted", "rows_scaled",
            "mix_done", "mix_out")
        y_done, y_squared, y_red, y_rooted, y_inverted, tok_made, x_put, gram_done, gram_out = sems(
            "y_done", "y_squared", "y_red", "y_rooted", "y_inverted", "tok_made", "x_put", "gram_done", "gram_out")
        z_turned, zb_made, zt_done, zt_out, zc_done, zc_out, z_squared, z_summed, zvar_done, z_rooted = sems(
            "z_turned", "zb_made", "zt_done", "zt_out", "zc_done", "zc_out", "z_squared", "z_summed", "zvar_done",
            "z_rooted")
        z_inverted, h1_done, h1_scaled, h1_summed, h1_out, h2_done, h2_out, out_done, out_put, stored = sems(
            "z_inverted", "h1_done", "h1_scaled", "h1_summed", "h1_out", "h2_done", "h2_out", "out_done", "out_put",
            "stored")

        block = ctx.enter_context(nc.Block())

        def back(t, m, k):
            return (t, m - k) if k <= m else (t - 1, m - k + CHUNKS)

        def real(t, m=0):
            return not isinstance(t, int) or 0 <= t < TILES

        def n(t, m=0):
            return CHUNKS * t + m + 1

        def free_after(eng, sem, count):
            if not isinstance(count, int) or count > 0:
                eng.wait_ge(sem, count)

        def places(t):
            last = isinstance(t, int) and t == TILES - 1
            return (p_mix, p_rt, zc_last, h1_last) if last else (p_a, p_b, zc_loop, h1_loop)

        def chunk_cols(g, m):
            lo = max(FIRST_EX[g], EX * m)
            hi = min((P * g + P - 1) // N_SP, EX * m + EX - 1) + 1
            return (lo - EX * m) * PROJ, (hi - EX * m) * PROJ, lo - FIRST_EX[g], hi - FIRST_EX[g]

        @block.sync
        def _(sp):
            sp.dma_start(ids_sb[:, :, :], ids).then_inc(ids_in, 16)
            sp.dma_start(F[:, :], first).then_inc(first_in, 16)
            sp.dma_start(wd[:, :, :], w_dense).then_inc(wd_in, 16)
            sp.dma_start(dn[:, :, :], dense).then_inc(dn_in, 16)
            sp.dma_start(A[:, :], setup_a).then_inc(a_in, 16)
            sp.dma_start(w1_d[:, :, :], w_top1_dense).then_inc(w1_d_in, 16)
            sp.dma_start(B[:, :], setup_b).then_inc(b_in, 16)
            sp.dma_start(wp[:, :, :], w_pairs).then_inc(wp_in, 16)
            sp.dma_start(wx[:, :], w_dense_token).then_inc(wp_in, 16)
            sp.wait_ge(gathered[0], 32 * len(PAIRS[0]))
            for k in range(3):
                sp.dma_start(w1[:, k, :], w_top1[:, k, :]).then_inc(w1_in, 16)
            for k in range(HT // 2):
                sp.dma_start(w2[:, 2 * k:2 * k + 2, :], w_top2[:, 2 * k:2 * k + 2, :]).then_inc(w2_in, 16)
            sp.wait_ge(out_put, TILES)
            sp.dma_start(out, y_sb[:, :]).then_inc(stored, 16)
            sp.wait_ge(stored, 16)

        @block.gpsimd
        def _(pool):
            pool.wait_ge(ids_in, 16)
            pool.tensor_tensor(idx[:, :, :], ids_sb[:, 0:TILES, :],
                               ids_sb[:, TILES:TILES + 1, :].broadcast_to([P, TILES, 2 * GROUPS]), ALU.add)\
                .then_inc(idx_made, 1)
            pool.wait_ge(idx_made, 1)
            for t in range(TILES):
                for m in range(CHUNKS):
                    if t:
                        pool.wait_ge(mix_done, n(t - 1, min(m + 1, CHUNKS - 1)))
                    for g in PAIRS[m]:
                        for half in range(2):
                            c = half * GROUPS + g
                            pool.indirect_dma_start(
                                out=rows[:, g, half, :], out_offset=None, in_=table,
                                in_offset=bass.IndirectOffsetOnAxis(ap=idx[:, t, c:c + 1], axis=0))\
                                .then_inc(gathered[m], 16)

        @block.tensor
        def _(pe):
            pe.wait_ge(ones_made, 1)
            pe.wait_ge(first_in, 16)
            pe.matmul(p_rt[:, 0:P], centre, ws2, start=True, stop=True)
            pe.matmul(p_rt[:, P:2 * P], ws2, centre, start=True, stop=True).then_inc(ws_centred, 1)
            pe.wait_ge(wsi_ready, 1)
            pe.matmul(p_q[D_SP:D_SP + 1, 0:PROJ], ones[0:N_SP, 0:1], wsi_c[:, :], start=True, stop=True)\
                .then_inc(col_sums, 1)
            pe.wait_ge(wd_ready, 1)
            pe.wait_ge(dn_in, 16)
            for k in range(2):
                mm = pe.matmul(p_a[:, :], wd[:, k, :], dn[:, k, :], start=(k == 0), stop=(k == 1))
            mm.then_inc(x_proj, 1)
            pe.wait_ge(wsc_ready, 1)
            pe.matmul(p_mix[:, 0:P], wsc[:, :], wsc[:, :], start=True, stop=True).then_inc(ws_ws, 1)
            pe.wait_ge(x_squared, 1)
            pe.matmul(p_b[:, :], ones[:, :], x_sq[:, :], start=True, stop=True).then_inc(x_var, 1)

            def dense_share(h):
                at = {0: p_y[:, 0:BATCH], 1: p_y[:, BATCH:2 * BATCH], 2: p_g[:, :], 3: p_b[:, :]}[h]
                pe.wait_ge(w1_d_in, 16)
                if h == 3:
                    pe.wait_ge(x_rooted, 1)
                for k in range(2):
                    mm = pe.matmul(at, w1_d[:, k, h * P:(h + 1) * P], dn[:, k, :], start=(k == 0), stop=(k == 1))
                mm.then_inc(dense_done, 1)

            def extra_weights(chunks):
                pe.wait_ge(select_ready, 1)
                pe.wait_ge(bias_ready, 1)
                pe.wait_ge(wp_in, 32)
                for c in chunks:
                    pe.matmul(p_b[0:EXTRA, :], m_sel[:, c, :], wp[:, c, :], start=(c == 0), stop=False)
                if PAIR_CHUNKS - 1 in chunks:
                    pe.matmul(p_b[0:EXTRA, :], m_x[:, :], wx[:, :], start=False, stop=True).then_inc(extra_done, 1)

            def top_bias():
                pe.wait_ge(dense_out, HT)
                pe.wait_ge(b_in, 16)
                pe.wait_ge(w1_in, 48)
                for k in range(3):
                    mm = pe.matmul(p_b[0:1, :], bl[:, k:k + 1], w1[:, k, :], start=(k == 0), stop=(k == 2))
                mm.then_inc(bias_done, 1)

            def turn_bias():
                pe.wait_ge(bias_out, 1)
                for h in range(HT):
                    mm = pe.matmul(p_b[:, h * P:(h + 1) * P], bias_row[:, h * P:(h + 1) * P], ones[0:1, :],
                                   start=True, stop=True)
                mm.then_inc(bias_turned, 1)

            def transpose_rows(t, m):
                pe.wait_ge(gathered[m], 32 * len(PAIRS[m]) * (t + 1))
                for i, g in enumerate(PAIRS[m]):
                    mm = pe.transpose(p_rt[:, i * P:(i + 1) * P],
                                      rows[:, g, :, :].rearrange("p h d -> p (h d)"), ident)
                mm.then_inc(rt_done, 1)

            def quad_rows(t, m):
                pe.wait_ge(rt_out, n(t, m))
                for i in range(len(PAIRS[m])):
                    mm = pe.matmul(p_q[:, i * P:(i + 1) * P], rows_t[:, i, :], quad[:, :], start=True, stop=True)
                mm.then_inc(q_done, 1)

            def mix_tables(t, m):
                pe.wait_ge(rows_scaled, n(t, m))
                for i, g in enumerate(NEEDS[m]):
                    lo, hi, j0, j1 = chunk_cols(g, m)
                    mm = pe.matmul(p_mix[:, lo:hi], rows[:, g, :, :].rearrange("p h d -> p (h d)"),
                                   proj[:, g, j0:j1, :], start=(i == 0), stop=(i == len(NEEDS[m]) - 1),
                                   skip_group_check=True)
                mm.then_inc(mix_done, 1)

            def widen(t, m):
                for half in range(2):
                    pe.wait_ge(mix_out, 2 * n(t, m) - 1 + half)
                    free_after(pe, tok_made, 2 * n(t, m) - 3 + half)
                    pe.matmul(p_y[:, half * COLS:(half + 1) * COLS], ws_g[:, :],
                              mix[:, half, :, :].rearrange("p b q -> p (b q)"), start=True, stop=True)\
                        .then_inc(y_done, 1)

            def token_products(t, m):
                pe.wait_ge(tok_made, 2 * n(t, m))
                pe.wait_ge(x_put, n(t, m))
                free_after(pe, gram_out, n(t, m) - 1)
                for b in range(2 * EX):
                    j, s = b % 4, (EX // 4) * (b // EX) + b % EX // 4
                    mm = pe.matmul(p_g[32 * j:32 * j + 32, s * GRAM:(s + 1) * GRAM], tok[:, m % 2, b, 2:GRAM],
                                   tok[:, m % 2, b, :], start=True, stop=True)
                mm.then_inc(gram_done, 1)

            def turn_features(t):
                to, to_b, _, _ = places(t)
                pe.wait_ge(zb_made, t + 1)
                if isinstance(t, int) and t == 0:
                    pe.wait_ge(wf_ready, 1)
                if to is p_a:
                    free_after(pe, out_put, t)
                pe.transpose(to_b[0:EXTRA, 0:P], zb[:, 0:EXTRA], ident)
                pe.matmul(to_b[0:1, 0:P], ones[:, 0:1], xt[:, bass.ds(t * P, P)], start=True, stop=True)
                for c in range(PAIR_CHUNKS):
                    mm = pe.transpose(to[:, c * P:(c + 1) * P], zp[:, c * P:(c + 1) * P], ident)
                mm.then_inc(zt_done, 1)

            def interact(t, blocks=range(4)):
                to, _, _, _ = places(t)
                pe.wait_ge(zt_out, t + 1)
                if isinstance(t, int) and t == 0:
                    pe.wait_ge(pairs_ready, PAIR_CHUNKS)
                for o in blocks:
                    for c in range(PAIR_CHUNKS):
                        pe.matmul(to[:, o * P:(o + 1) * P], wp[:, c, o * P:(o + 1) * P], zt[:, c, :],
                                  start=(c == 0), stop=False)
                    mm = pe.matmul(to[:, o * P:(o + 1) * P], wf[:, o * P:(o + 1) * P],
                                   zt[0:EXTRA, PAIR_CHUNKS, :], start=False, stop=True)
                if 3 in blocks:
                    mm.then_inc(zc_done, 1)

            def feature_variance(t):
                _, to_b, _, _ = places(t)
                pe.wait_ge(z_summed, t + 1)
                pe.matmul(to_b[:, 0:P], ones[:, :], z_sum[:, :], start=True, stop=True).then_inc(zvar_done, 1)

            def top1(t, blocks=range(HT)):
                to, _, zc, _ = places(t)
                pe.wait_ge(zc_out, t + 1)
                for h in blocks:
                    for k in range(3):
                        mm = pe.matmul(to[:, h * P:(h + 1) * P], w1[:, k, h * P:(h + 1) * P], zc[:, k, :],
                                       start=(k == 0), stop=(k == 2))
                if HT - 1 in blocks:
                    mm.then_inc(h1_done, 1)

            def top2(t, blocks=range(H2 // P)):
                _, to_b, _, h1 = places(t)
                pe.wait_ge(h1_out, t + 1)
                for o in blocks:
                    for k in range(HT):
                        mm = pe.matmul(to_b[:, o * P:(o + 1) * P], w2[:, k, o * P:(o + 1) * P], h1[:, k, :],
                                       start=(k == 0), stop=(k == HT - 1))
                if H2 // P - 1 in blocks:
                    mm.then_inc(h2_done, 1)

            def top3(t):
                to, _, _, _ = places(t)
                pe.wait_ge(h2_out, t + 1)
                for k in range(H2 // P):
                    mm = pe.matmul(to[0:1, 0:P], w3[:, k:k + 1], h2[:, k, :], start=(k == 0), stop=(k == 1))
                mm.then_inc(out_done, 1)

            def step(t, m):
                before, third = back(t, m, 1), back(t, m, 3)
                if real(t):
                    transpose_rows(t, m)
                if m == 0 and isinstance(t, int) and t == 0:
                    dense_share(2)
                if real(*before):
                    mix_tables(*before)
                if m == 1 and real(t - 2):
                    feature_variance(t - 2)
                if m == 0 and real(t - 2):
                    interact(t - 2, [1, 2, 3])
                if m == 2 and real(t - 2):
                    top2(t - 2)
                if real(t):
                    quad_rows(t, m)
                if real(*third):
                    token_products(*third)
                if m == 3 and real(t - 1):
                    turn_features(t - 1)
                if m == 1 and real(t - 2):
                    top1(t - 2)
                if m == 2 and real(t - 2):
                    top3(t - 2)
                if real(*before):
                    widen(*before)
                if m == 3 and real(t - 1):
                    interact(t - 1, [0])

            dense_share(0)
            pe.wait_ge(a_in, 16)
            pe.wait_ge(quad_ready, 1)
            pe.wait_ge(bs_ready, 1)
            pe.wait_ge(proj_ready, 1)
            dense_share(1)
            step(0, 0)
            dense_share(3)
            pe.wait_ge(dense_out, 2)
            step(0, 1)
            top_bias()
            pe.wait_ge(proj_ready, 2)
            step(0, 2)
            turn_bias()
            step(0, 3)
            extra_weights([0, 1])
            step(1, 0)
            extra_weights([2, 3])
            step(1, 1)
            step(1, 2)
            pe.wait_ge(x_ready, TILES)
            step(1, 3)
            pe.wait_ge(top_ready, 3)
            pe.wait_ge(w2_in, 32)
            with pe.Fori(2, TILES) as t:
                for m in range(CHUNKS):
                    step(t, m)
            t, u = TILES - 1, TILES - 2
            mix_tables(t, 3)
            token_products(t, 1)
            widen(t, 3)
            token_products(t, 2)
            interact(u, [1, 2])
            token_products(t, 3)
            interact(u, [3])
            top1(u, [0, 1])
            turn_features(t)
            feature_variance(u)
            top1(u, [2, 3])
            interact(t)
            top2(u, [0])
            top1(t, [0, 1])
            feature_variance(t)
            top1(t, [2, 3])
            top2(u, [1])
            top3(u)
            top2(t)
            top3(t)

        @block.scalar
        def _(act):
            act.wait_ge(first_in, 16)
            act.activation(q_std[:, 0, 0:1], eps, ACT.Sqrt)
            act.wait_ge(x_proj, 1)
            act.activation(x_sq[:, :], p_a[:, :], ACT.Square, scale=float(E) ** -0.5).then_inc(x_squared, 1)
            act.wait_ge(x_var, 1)
            act.activation(x_std[:, :], p_b[:, :], ACT.Sqrt, bias=eps).then_inc(x_rooted, 1)

            def rows_out(t, m):
                act.wait_ge(rt_done, n(t, m))
                w = len(PAIRS[m]) * P
                act.activation(rows_t[:, 0:len(PAIRS[m]), :], p_rt[:, 0:w], ACT.Copy).then_inc(rt_out, 1)

            def mix_move(t, m):
                act.wait_ge(mix_done, n(t, m))
                for half in range(2):
                    act.activation(mix[0:D_SP, half, :, :].rearrange("p b q -> p (b q)"),
                                   p_mix[half * D_SP:(half + 1) * D_SP, :], ACT.Copy).then_inc(mix_out, 1)

            def row_root(t, m):
                act.wait_ge(q_red, n(t, m))
                k = len(PAIRS[m])
                act.activation(q_std[:, 0:k, :], q_var[:, 0:k, :], ACT.Sqrt, bias=eps).then_inc(q_rooted, 1)

            def gram_move(t, m):
                if m == 0:
                    free_after(act, zb_made, t)
                act.wait_ge(gram_done, n(t, m))
                act.activation(grams[:, :, m * SLOTS:(m + 1) * SLOTS].rearrange("p c s -> p s c"),
                               p_g[:, 0:SLOTS * GRAM].rearrange("p (s c) -> p s c", c=GRAM),
                               ACT.Copy).then_inc(gram_out, 1)

            def put_dense_token(t, m):
                if isinstance(t, int):
                    act.wait_ge(x_ready, t + 1)
                src = xt[:, bass.ds(t * P, P)].rearrange("p (j s) -> p s j", j=4)[:, m * SLOTS:(m + 1) * SLOTS, :]
                act.activation(tok[:, m % 2, :, 0].rearrange("p (s j) -> p s j", j=4), src, ACT.Copy)\
                    .then_inc(x_put, 1)

            def square(t, m):
                for half in range(2):
                    act.wait_ge(y_done, 2 * n(t, m) - 1 + half)
                    act.activation(sq[:, half * COLS:(half + 1) * COLS], p_y[:, half * COLS:(half + 1) * COLS],
                                   ACT.Square, scale=float(PROJ) ** -0.5).then_inc(y_squared, 1)

            def token_root(t, m):
                act.wait_ge(y_red, 2 * n(t, m))
                act.activation(y_std[:, :], y_var[:, :], ACT.Sqrt, bias=eps).then_inc(y_rooted, 1)

            def dense_move(h):
                act.wait_ge(dense_done, h + 1)
                at = {0: p_y[:, 0:BATCH], 1: p_y[:, BATCH:2 * BATCH], 2: p_g[:, :], 3: p_b[:, :]}[h]
                act.activation(h1_dense[:, h, :], at, ACT.Copy).then_inc(dense_out, 1)

            def centre_extra():
                act.wait_ge(extra_mean, 1)
                act.activation(wf[:, :], p_b[0:EXTRA, :], ACT.Identity, bias=less_mean_x).then_inc(wf_ready, 1)

            def scale_pairs(c):
                act.wait_ge(pair_means, 1)
                act.wait_ge(extra_done, 1)
                act.activation(wp[:, c, :], wp[:, c, :], ACT.Identity, bias=less_mean[:, c:c + 1],
                               scale=aa[:, c:c + 1]).then_inc(pairs_ready, 1)

            def bias_move():
                act.wait_ge(bias_done, 1)
                act.activation(bias_row[:, :], p_b[0:1, :], ACT.Copy).then_inc(bias_out, 1)

            def add_bias(h):
                act.wait_ge(bias_ready, 1)
                act.activation(h1_dense[:, h, :], h1_dense[:, h, :], ACT.Identity, bias=bias1[:, h:h + 1])\
                    .then_inc(share_ready, 1)

            def scale_top(k):
                act.wait_ge(bias_done, 1)
                act.activation(w1[:, k, :], w1[:, k, :], ACT.Copy, scale=gl[:, k:k + 1]).then_inc(top_ready, 1)

            def features_out(t):
                to, to_b, _, _ = places(t)
                act.wait_ge(zt_done, t + 1)
                act.activation(zt[:, 0:PAIR_CHUNKS, :], to[:, :], ACT.Copy)
                act.activation(zt[0:EXTRA, PAIR_CHUNKS, :], to_b[0:EXTRA, 0:P], ACT.Copy).then_inc(zt_out, 1)

            def interactions_out(t):
                to, _, zc, _ = places(t)
                act.wait_ge(zc_done, t + 1)
                act.activation(zc[:, :, :], to[:, :], ACT.Copy).then_inc(zc_out, 1)
                act.wait_ge(zc_out, t + 1)
                act.activation(z_sq[:, :, :], zc[:, :, :], ACT.Square, scale=float(MAXD) ** -0.5).then_inc(z_squared, 1)

            def feature_root(t):
                _, to_b, _, _ = places(t)
                act.wait_ge(zvar_done, t + 1)
                act.activation(z_std[:, :], to_b[:, 0:P], ACT.Sqrt, bias=eps).then_inc(z_rooted, 1)

            def relu1(t):
                _, _, _, h1 = places(t)
                act.wait_ge(h1_summed, t + 1)
                act.activation(h1[:, :, :], h1_pre[:, :, :], ACT.Relu).then_inc(h1_out, 1)

            def relu2(t):
                _, to_b, _, _ = places(t)
                act.wait_ge(h2_done, t + 1)
                for o in range(H2 // P):
                    i = act.activation(h2[:, o, :], to_b[:, o * P:(o + 1) * P], ACT.Relu, bias=b2[:, o:o + 1])
                i.then_inc(h2_out, 1)

            def outputs(t):
                to, _, _, _ = places(t)
                act.wait_ge(out_done, t + 1)
                act.activation(y_sb[:, bass.ds(t * P, P)], to[0:1, 0:P], ACT.Copy).then_inc(out_put, 1)

            def step(t, m, early=None, between=None):
                before, second, third = (back(t, m, k) for k in (1, 2, 3))
                if real(t):
                    rows_out(t, m)
                if m == 0 and isinstance(t, int) and t == 0:
                    dense_move(2)
                if m == 1 and real(t - 2):
                    feature_root(t - 2)
                if real(*second):
                    token_root(*second)
                if real(*before):
                    mix_move(*before)
                if m == 0 and real(t - 2):
                    interactions_out(t - 2)
                if m == 2 and real(t - 2):
                    relu2(t - 2)
                if m == 3 and real(t - 1):
                    features_out(t - 1)
                if early:
                    early()
                if real(t):
                    row_root(t, m)
                if real(*third):
                    gram_move(*third)
                if m == 2 and real(t - 2):
                    outputs(t - 2)
                if between:
                    between()
                if real(*before):
                    put_dense_token(*before)
                    square(*before)
                if m == 1 and real(t - 2):
                    relu1(t - 2)

            dense_move(0)
            dense_move(1)
            step(0, 0)
            step(0, 1, lambda: dense_move(3))
            bias_move()
            step(0, 2, lambda: scale_top(0), lambda: scale_top(1))
            step(0, 3, lambda: scale_top(2), lambda: add_bias(0))
            step(1, 0, lambda: add_bias(1))
            step(1, 1, lambda: scale_pairs(0), lambda: scale_pairs(1))
            step(1, 2, centre_extra, lambda: scale_pairs(2))
            step(1, 3, lambda: scale_pairs(3), lambda: [add_bias(2), add_bias(3)])
            with act.Fori(2, TILES) as t:
                for m in range(CHUNKS):
                    step(t, m)
            t, u = TILES - 1, TILES - 2
            token_root(t, 2)
            mix_move(t, 3)
            gram_move(t, 1)
            put_dense_token(t, 3)
            square(t, 3)
            gram_move(t, 2)
            token_root(t, 3)
            gram_move(t, 3)
            interactions_out(u)
            features_out(t)
            feature_root(u)
            relu1(u)
            interactions_out(t)
            feature_root(t)
            relu2(u)
            relu1(t)
            outputs(u)
            relu2(t)
            outputs(t)

        @block.vector
        def _(dve):
            steps = [0]

            def done(i):
                steps[0] += 1
                i.then_inc(dve_step, 1)
                dve.wait_ge(dve_step, steps[0])

            dve.memset(ones[:, :], 1.0).then_inc(ones_made, 1)
            dve.memset(tok[:, :, :, 1], 1.0)
            dve.memset(zb[:, 0:1], 0.0)
            done(dve.memset(zb[:, 1:2], 1.0))
            dve.wait_ge(first_in, 16)
            mean_t, mean_r = small[0:N_SP, 0:1], small[:, 8:8 + GROUPS]
            done(dve.tensor_reduce(mean_t, wsi_t, AX.X, ALU.add))
            done(dve.tensor_scalar(mean_t, mean_t, 1.0 / PROJ, None, ALU.mult))
            dve.tensor_scalar(wsi_c[:, :], wsi_t, mean_t, None, ALU.subtract).then_inc(wsi_ready, 1)
            dve.wait_ge(wd_in, 16)
            mean_d = small[:, 24:26]
            done(dve.tensor_reduce(mean_d, wd[:, :, :], AX.X, ALU.add))
            done(dve.tensor_scalar(mean_d, mean_d, 1.0 / E, None, ALU.mult))
            dve.tensor_tensor(wd[:, :, :], wd[:, :, :], mean_d.unsqueeze(2).broadcast_to([P, 2, E]),
                              ALU.subtract).then_inc(wd_ready, 1)
            dve.wait_ge(ws_centred, 1)
            dve.tensor_copy(wsc[:, :], p_rt[:, 0:P]).then_inc(wsc_ready, 1)
            dve.wait_ge(a_in, 16)
            dve.tensor_tensor(ws_g[0:D_SP, :], p_rt[0:D_SP, P:2 * P], gs_row[0:D_SP, :], ALU.mult)
            done(dve.tensor_reduce(mean_r, wsi_rows, AX.X, ALU.add))
            done(dve.tensor_scalar(mean_r, mean_r, 1.0 / PROJ, None, ALU.mult))
            done(dve.tensor_tensor(wsi_rows, wsi_rows, mean_r.unsqueeze(2).broadcast_to([P, GROUPS, PROJ]),
                                   ALU.subtract))

            def make_proj(g0, g1):
                wide = [P, g1 - g0, SPAN, PROJ]
                dve.tensor_tensor(proj[:, g0:g1, :, :], wsi_rows[:, g0:g1, :].unsqueeze(2).broadcast_to(wide),
                                  own[:, g0:g1, :].unsqueeze(3).broadcast_to(wide), ALU.mult).then_inc(proj_ready, 1)

            make_proj(0, LAST_OF[0] + 1)
            dve.wait_ge(ws_ws, 1)
            dve.tensor_tensor(quad[:, :], p_mix[:, 0:P], same_half, ALU.mult).then_inc(quad_ready, 1)
            dve.tensor_copy(ws_g[D_SP:D_SP + 1, :], bs_row)
            dve.wait_ge(col_sums, 1)
            for half in range(2):
                i = dve.tensor_copy(mix[D_SP:D_SP + 1, half, :, :],
                                    p_q[D_SP:D_SP + 1, 0:PROJ].unsqueeze(1).broadcast_to([1, EX, PROJ]))
            i.then_inc(bs_ready, 1)

            def dense_token(t):
                at = slice(t * P, (t + 1) * P)
                dve.wait_ge(x_rooted, 1)
                done(dve.reciprocal(xt[:, at], x_std[:, at]))
                done(dve.tensor_tensor(xt[:, at], xt[:, at], p_a[:, at], ALU.mult))
                dve.tensor_scalar(xt[:, at], xt[:, at], gd, bd, ALU.mult, ALU.add).then_inc(x_ready, 1)

            def selectors():
                dve.wait_ge(b_in, 16)
                dve.tensor_tensor(ac, gb[:, 0, :], gb[:, 3, :], ALU.mult)
                dve.tensor_tensor(ca, gb[:, 1, :], gb[:, 2, :], ALU.mult)
                dve.tensor_tensor(cc, gb[:, 2, :], gb[:, 3, :], ALU.mult)
                done(dve.tensor_tensor(aa, gb[:, 0, :], gb[:, 1, :], ALU.mult))
                wide = [P, PAIR_CHUNKS, EXTRA]
                done(dve.tensor_tensor(m_sel[:, :, :], hot[:, 0, :, :], ac.unsqueeze(2).broadcast_to(wide), ALU.mult))
                for w, s in ((1, ca), (2, cc)):
                    done(dve.tensor_tensor(m_tmp[:, :, :], hot[:, w, :, :], s.unsqueeze(2).broadcast_to(wide),
                                           ALU.mult))
                    done(dve.tensor_tensor(m_sel[:, :, :], m_sel[:, :, :], m_tmp[:, :, :], ALU.add))
                done(dve.tensor_scalar(m_x[:, :], hot_x[:, 0, :], gb_x[:, 0:1], None, ALU.mult))
                dve.scalar_tensor_tensor(out=m_x[:, :], in0=hot_x[:, 1, :], scalar=gb_x[:, 1:2], in1=m_x[:, :],
                                         op0=ALU.mult, op1=ALU.add).then_inc(select_ready, 1)

            def pair_sums(chunks):
                dve.wait_ge(wp_in, 32)
                for c in chunks:
                    i = dve.tensor_reduce(row_sum[:, c:c + 1], wp[:, c, :], AX.X, ALU.add)
                if PAIR_CHUNKS - 1 in chunks:
                    done(i)
                    dve.scalar_tensor_tensor(out=less_mean, in0=row_sum, scalar=-1.0 / MAXD, in1=aa, op0=ALU.mult,
                                             op1=ALU.mult).then_inc(pair_means, 1)

            def extra_sums():
                dve.wait_ge(extra_done, 1)
                done(dve.tensor_reduce(row_sum_x, p_b[0:EXTRA, :], AX.X, ALU.add))
                dve.tensor_scalar(less_mean_x, row_sum_x, -1.0 / MAXD, None, ALU.mult).then_inc(extra_mean, 1)

            def finish_bias():
                dve.wait_ge(bias_turned, 1)
                dve.tensor_tensor(bias1[:, :], p_b[:, :].rearrange("p (h c) -> p h c", c=P)[:, :, 0], b1, ALU.add)\
                    .then_inc(bias_ready, 1)

            def scale_rows(t, m):
                k, g0 = len(PAIRS[m]), PAIRS[m][0]
                here = rows[:, g0:g0 + k, :, :]
                dve.wait_ge(q_done, n(t, m))
                dve.tensor_tensor(prod[:, 0:k, :, :], p_q[:, 0:k * P].rearrange("p (g h d) -> p g h d", h=2, d=D_SP),
                                  here, ALU.mult).then_inc(prod_done, 1)
                dve.wait_ge(prod_done, n(t, m))
                dve.tensor_reduce(q_var[:, 0:k, :], prod[:, 0:k, :, :], AX.X, ALU.add).then_inc(q_red, 1)
                dve.wait_ge(q_rooted, n(t, m))
                dve.reciprocal(q_inv[:, 0:k, :], q_std[:, 0:k, :]).then_inc(q_inverted, 1)
                dve.wait_ge(q_inverted, n(t, m))
                dve.tensor_tensor(here, here, q_inv[:, 0:k, :].unsqueeze(3).broadcast_to([P, k, 2, D_SP]),
                                  ALU.mult).then_inc(rows_scaled, 1)

            def token_variance(t, m):
                for half in range(2):
                    dve.wait_ge(y_squared, 2 * n(t, m) - 1 + half)
                    dve.tensor_reduce(y_var[:, half * EX:(half + 1) * EX],
                                      sq[:, half * COLS:(half + 1) * COLS].rearrange("p (b q) -> p b q", q=PROJ),
                                      AX.X, ALU.add).then_inc(y_red, 1)

            def make_tokens(t, m):
                dve.wait_ge(y_rooted, n(t, m))
                dve.reciprocal(y_inv[:, :], y_std[:, :]).then_inc(y_inverted, 1)
                dve.wait_ge(y_inverted, n(t, m))
                free_after(dve, gram_done, n(t, m) - 2)
                for half in range(2):
                    b = slice(half * EX, (half + 1) * EX)
                    dve.tensor_tensor(tok[:, m % 2, b, 2:GRAM],
                                      p_y[:, half * COLS:(half + 1) * COLS].rearrange("p (b q) -> p b q", q=PROJ),
                                      y_inv[:, b].unsqueeze(2).broadcast_to([P, EX, PROJ]), ALU.mult)\
                        .then_inc(tok_made, 1)

            def features(t):
                dve.wait_ge(gram_out, n(t, CHUNKS - 1))
                free_after(dve, zt_done, t)
                dve.transpose(zb[:, 2:2 + GRAM * PROJ], grams[:, :, :].rearrange("p c s -> p (c s)"))\
                    .then_inc(z_turned, 1)

            def pair_features(t):
                dve.wait_ge(z_turned, 2 * t + 1)
                at = 2 + GRAM * PROJ
                dve.tensor_copy(zb[:, at:at + DUP * PROJ], zb[:, 2 + 2 * PROJ:2 + (2 + DUP) * PROJ])\
                    .then_inc(z_turned, 1)
                dve.wait_ge(z_turned, 2 * t + 2)
                base = zb[:, EXTRA + PROJ:EXTRA + PROJ + 1]
                diagonals = bass.AP(base.tensor, base.offset, [base.ap[0], [PROJ, PROJ // 2], [PROJ + 1, PROJ]])
                dve.tensor_copy(zp[:, :].rearrange("p (k q) -> p k q", q=PROJ), diagonals).then_inc(zb_made, 1)

            def sum_squares(t):
                dve.wait_ge(z_squared, t + 1)
                dve.tensor_reduce(z_sum[:, :], z_sq[:, :, :].rearrange("p o b -> p b o"), AX.X, ALU.add)\
                    .then_inc(z_summed, 1)

            def invert_deviation(t):
                dve.wait_ge(z_rooted, t + 1)
                dve.reciprocal(z_inv[:, :], z_std[:, :]).then_inc(z_inverted, 1)

            def first_layer(t):
                to, _, _, _ = places(t)
                dve.wait_ge(z_inverted, t + 1)
                dve.wait_ge(h1_done, t + 1)
                free_after(dve, h1_out, t)
                dve.tensor_tensor(h1_pre[:, :, :], to[:, :].rearrange("p (h b) -> p h b", h=HT),
                                  z_inv[:, :].unsqueeze(1).broadcast_to([P, HT, P]), ALU.mult).then_inc(h1_scaled, 1)
                dve.wait_ge(h1_scaled, t + 1)
                dve.tensor_tensor(h1_pre[:, :, :], h1_pre[:, :, :], h1_dense[:, :, bass.ds(t * P, P)], ALU.add)\
                    .then_inc(h1_summed, 1)

            def step(t, m, between=None):
                before, second = (back(t, m, k) for k in (1, 2))
                if real(*second):
                    make_tokens(*second)
                if m == 1 and real(t - 2):
                    invert_deviation(t - 2)
                if real(t):
                    scale_rows(t, m)
                if m == 0 and real(t - 2):
                    sum_squares(t - 2)
                if m == 1 and real(t - 2):
                    first_layer(t - 2)
                if m == 2 and real(t - 1):
                    features(t - 1)
                if between:
                    between()
                if real(*before):
                    token_variance(*before)
                if m == 2 and real(t - 1):
                    pair_features(t - 1)

            dve.wait_ge(b_in, 16)
            selectors()
            dense_token(0)
            dense_token(1)
            step(0, 0)
            make_proj(LAST_OF[0] + 1, GROUPS)
            dense_token(2)
            step(0, 1, lambda: pair_sums([0]))
            step(0, 2, finish_bias)
            step(0, 3, lambda: pair_sums([1, 2, 3]))
            step(1, 0, lambda: dense_token(3))
            step(1, 1, extra_sums)
            step(1, 2)
            step(1, 3)
            dve.wait_ge(share_ready, HT)
            with dve.Fori(2, TILES) as t:
                for m in range(CHUNKS):
                    step(t, m)
            t, u = TILES - 1, TILES - 2
            make_tokens(t, 2)
            token_variance(t, 3)
            make_tokens(t, 3)
            features(t)
            pair_features(t)
            sum_squares(u)
            invert_deviation(u)
            first_layer(u)
            sum_squares(t)
            invert_deviation(t)
            first_layer(t)


def kernel(**inputs):
    import concourse.bacc as bacc
    from concourse.bass_utils import run_bass_kernel_spmd

    x = {k: np.asarray(v) for k, v in inputs.items()}
    tables = [x[f"tbl_{k}"] for k in range(N_SP)]
    table = np.concatenate(tables, axis=0)
    starts = np.cumsum([0] + [t.shape[0] for t in tables[:-1]]).astype(np.int32)

    def cols(*parts):
        out = []
        for p in parts:
            p = np.asarray(p, np.float32).reshape(p.shape[0], -1)
            out.append(np.concatenate([p, np.zeros((P - p.shape[0], p.shape[1]), np.float32)]))
        return np.ascontiguousarray(np.concatenate(out, axis=1))

    def halves(v, k):
        return v.reshape(k, P).T

    flat = np.arange(GROUPS * P).reshape(GROUPS, P)
    of_table, of_example = flat % N_SP, flat // N_SP
    offsets = np.tile(starts[of_table].T, (1, 2))
    ids = x["ids"].reshape(TILES, 2 * GROUPS, P).transpose(2, 0, 1)
    ids = np.ascontiguousarray(np.concatenate([ids, offsets[:, None, :]], axis=1)).astype(np.int32)

    wsi, ws = x["L0_rec_Wsi"], x["L0_rec_Ws"]
    eye = np.eye(P, dtype=np.float32)
    half_of = np.arange(P) // D_SP
    own = (of_example.T[:, :, None] == np.array(FIRST_EX)[None, :, None] + np.arange(SPAN)).astype(np.float32)
    first_in = cols(eye - np.float32(1 / P), np.concatenate([ws, ws], axis=1), wsi.T,
                    np.full((P, 1), EPS, np.float32))
    setup_a = cols(eye, (half_of[:, None] == half_of) / np.float32(E), np.broadcast_to(x["L0_rec_gs"], (P, E)),
                   wsi.T[of_table.T], own, np.broadcast_to(x["L0_rec_bs"], (P, E)))

    first, second, k = feature_pairs()
    i, j = np.maximum(first, second) + 1, np.minimum(first, second) + 1
    twice = (k == PROJ // 2) & (first >= PROJ // 2)
    wl_t = x["L0_rec_Wl"].T
    w_pairs = wl_t[i * (i - 1) // 2 + j]
    w_pairs[twice] = 0
    w_pairs = np.ascontiguousarray(w_pairs.transpose(1, 0, 2))
    tok = np.arange(PROJ) + 1
    w_dense_token = np.ascontiguousarray(wl_t[tok * (tok - 1) // 2])

    gsi, bsi = x["L0_rec_gsi"], x["L0_rec_bsi"]
    gb = np.stack([gsi[first], gsi[second], bsi[first], bsi[second]]).transpose(2, 0, 1)
    hot = np.zeros((P, 3, PAIR_CHUNKS, EXTRA), np.float32)
    for c in range(PAIR_CHUNKS):
        hot[np.arange(P), 0, c, 2 + PROJ + first[c]] = 1
        hot[np.arange(P), 1, c, 2 + PROJ + second[c]] = 1
        hot[:, 2, c, 1] = E
    hot_x = np.zeros((PROJ, 2, EXTRA), np.float32)
    hot_x[np.arange(PROJ), 0, 2 + np.arange(PROJ)] = 1
    hot_x[:, 1, 0] = 1
    setup_b = cols(x["L0_rec_gd"][:, None], x["L0_rec_bd"][:, None], halves(x["L0_rec_gl"][:DIMS], 3),
                   halves(x["L0_rec_bl"][:DIMS], 3), halves(x["b_top1"], H1 // P), halves(x["b_top2"], H2 // P),
                   halves(x["W_top3"][:, 0], H2 // P), gb, np.stack([gsi, bsi], axis=1), hot, hot_x)

    w1 = x["W_top1"]
    w1, w1_dense = (w.reshape(-1, P, H1).transpose(1, 0, 2) for w in (w1[:DIMS], w1[MAXD:]))
    w2 = x["W_top2"].reshape(H1 // P, P, H2).transpose(1, 0, 2)
    order = example_order()
    dense = x["r_dense_t"].reshape(TILES, P, D_DENSE)[:, order].reshape(BATCH, 2, P).transpose(2, 1, 0)
    w_dense = x["L0_rec_Wd"].reshape(E, 2, P).transpose(2, 1, 0)

    arrays = {"table": table, "ids": ids, "first": first_in, "setup_a": setup_a, "setup_b": setup_b, "w_pairs": w_pairs,
              "w_dense_token": w_dense_token, "w_top1": w1, "w_top1_dense": w1_dense, "w_top2": w2,
              "dense": dense, "w_dense": w_dense}
    arrays = {f"in_{k}": np.ascontiguousarray(v) for k, v in arrays.items()}
    nc = bacc.Bacc("TRN2", target_bir_lowering=False, num_devices=1)
    args = [nc.dram_tensor(k, v.shape, mybir.dt.from_np(v.dtype), kind="ExternalInput").ap()
            for k, v in arrays.items()]
    out = nc.dram_tensor("out_y", (1, BATCH), mybir.dt.float32, kind="ExternalOutput").ap()
    dlrm_tower(nc, *args, out)
    r = run_bass_kernel_spmd(nc, [arrays], core_ids=[0])
    y = r.results[0]["out_y"].reshape(TILES, P)
    got = np.zeros((TILES, P), np.float32)
    got[:, order] = y
    return got.reshape(BATCH, 1)
```
